# Optimizing a Trainium2 kernel written in Bass

```python
import numpy as np
import jax
import jax.numpy as jnp

def _softmax(x, axis=-1):
    return jax.nn.softmax(x, axis=axis)

def _gelu(x):
    return jax.nn.gelu(x, approximate=True)

def _silu(x):
    return jax.nn.silu(x)

def _sigmoid(x):
    return jax.nn.sigmoid(x)

def _layernorm(x, axis=-1, eps=1e-05):
    m = jnp.mean(x, axis=axis, keepdims=True)
    v = jnp.var(x, axis=axis, keepdims=True)
    return (x - m) / jnp.sqrt(v + eps)

def _scatter_add(tgt, idx, src, axis=0):
    return tgt.at[idx].add(src)

def _segment_sum(src, seg, n):
    return jax.ops.segment_sum(src, seg, n)
kernel_name = 'mk_seq_postln_d1_jaxref_r8_01cee5'

def setup_inputs(seed: int=0):
    np.random.seed(seed)
    _w = jnp.asarray

    def _L0_attn_setup():
        import jax, jax.numpy as jnp
        import numpy as np
        H, NS = (16, 8)
        key = jax.random.key(seed)
        ks = jax.random.split(key, 8)
        B, S, Dm = (1, 256, 256)
        hd = Dm // H
        return {'hidden_states': jax.random.normal(ks[0], (B, S, Dm), jnp.float32), 'Wq': jax.random.normal(ks[1], (Dm, Dm), jnp.float32) * 0.02, 'Wk': jax.random.normal(ks[2], (Dm, Dm), jnp.float32) * 0.02, 'Wv': jax.random.normal(ks[3], (Dm, Dm), jnp.float32) * 0.02, 'Wo': jax.random.normal(ks[4], (Dm, Dm), jnp.float32) * 0.02, 'splat_positions': jax.random.normal(ks[5], (H, NS, hd), jnp.float32) * 0.02, 'splat_directions': jax.random.normal(ks[6], (H, NS, hd), jnp.float32) * 0.02, 'splat_log_scales': jnp.full((H, NS), np.float32(np.log(0.8)), jnp.float32), 'splat_log_amplitudes': jnp.full((H, NS), np.float32(-np.log(NS)), jnp.float32), 'directional_strength': jnp.float32(0.4), 'position_sensitivity': jnp.float32(0.3), 'gsa_strength': jnp.float32(-4.0)}
    _L0_attn_in = _L0_attn_setup()

    def _L0_ffn_setup():
        import jax, jax.numpy as jnp
        import numpy as np

        def _sparsify_2to4(h):
            B, S, I = h.shape
            g = h.reshape(B, S, I // 4, 4)
            a = jnp.abs(g)
            _, idx = jax.lax.top_k(a, 2)
            pos = jnp.arange(4)
            mask = (pos == idx[..., 0:1]) | (pos == idx[..., 1:2])
            return (g * mask.astype(g.dtype)).reshape(B, S, I)
        key = jax.random.key(seed)
        k1, k2, k3, k4 = jax.random.split(key, 4)
        B, S, H, I = (4, 256, 256, 1024)
        x = jax.random.normal(k1, (B, S, H), dtype=jnp.float32)
        w_gate = jax.random.normal(k2, (H, I), dtype=jnp.float32) / np.sqrt(H)
        w_up = jax.random.normal(k3, (H, I), dtype=jnp.float32) / np.sqrt(H)
        w_down = jax.random.normal(k4, (I, H), dtype=jnp.float32) / np.sqrt(I)
        return {'x': x, 'w_gate': w_gate, 'w_up': w_up, 'w_down': w_down}
    _L0_ffn_in = _L0_ffn_setup()
    _d = {'L0_attn_hidden_states': _L0_attn_in['hidden_states'], 'L0_attn_Wq': _L0_attn_in['Wq'], 'L0_attn_Wk': _L0_attn_in['Wk'], 'L0_attn_Wv': _L0_attn_in['Wv'], 'L0_attn_Wo': _L0_attn_in['Wo'], 'L0_attn_splat_positions': _L0_attn_in['splat_positions'], 'L0_attn_splat_directions': _L0_attn_in['splat_directions'], 'L0_attn_splat_log_scales': _L0_attn_in['splat_log_scales'], 'L0_attn_splat_log_amplitudes': _L0_attn_in['splat_log_amplitudes'], 'L0_attn_directional_strength': _L0_attn_in['directional_strength'], 'L0_attn_position_sensitivity': _L0_attn_in['position_sensitivity'], 'L0_attn_gsa_strength': _L0_attn_in['gsa_strength'], 'L0_ffn_w_gate': _L0_ffn_in['w_gate'], 'L0_ffn_w_up': _L0_ffn_in['w_up'], 'L0_ffn_w_down': _L0_ffn_in['w_down']}
    _x0 = _d['L0_attn_hidden_states']
    _d['L0_attn_hidden_states'] = jax.random.normal(jax.random.fold_in(jax.random.key(seed), 1), (1, 1024, 256), dtype=_x0.dtype)
    del _x0
    return _d

def reference(L0_attn_hidden_states, L0_attn_Wq, L0_attn_Wk, L0_attn_Wv, L0_attn_Wo, L0_attn_splat_positions, L0_attn_splat_directions, L0_attn_splat_log_scales, L0_attn_splat_log_amplitudes, L0_attn_directional_strength, L0_attn_position_sensitivity, L0_attn_gsa_strength, L0_ffn_w_gate, L0_ffn_w_up, L0_ffn_w_down):

    def _L0_attn_ref(hidden_states, Wq, Wk, Wv, Wo, splat_positions, splat_directions, splat_log_scales, splat_log_amplitudes, directional_strength, position_sensitivity, gsa_strength):
        import jax, jax.numpy as jnp
        import numpy as np
        H, NS = (16, 8)
        B, S, Dm = hidden_states.shape
        Hn, Ns, hd = splat_positions.shape

        def heads(x):
            return x.reshape(B, S, Hn, hd).transpose(0, 2, 1, 3)
        q = heads(hidden_states @ Wq.T)
        k = heads(hidden_states @ Wk.T)
        v = heads(hidden_states @ Wv.T)
        scores = jnp.einsum('bhid,bhjd->bhij', q, k) / jnp.sqrt(jnp.float32(hd))
        mask = jnp.tril(jnp.ones((S, S), bool))
        neg = jnp.finfo(scores.dtype).min

        def out_proj(attn):
            o = jnp.einsum('bhij,bhjd->bhid', attn, v)
            return o.transpose(0, 2, 1, 3).reshape(B, S, Dm) @ Wo.T
        std_out = out_proj(jax.nn.softmax(jnp.where(mask, scores, neg), axis=-1))
        scales = jnp.exp(splat_log_scales)
        amps = jnp.exp(splat_log_amplitudes)
        dirn = splat_directions / (jnp.linalg.norm(splat_directions, axis=-1, keepdims=True) + 1e-08)

        def splat_feats(x):
            diff = x[:, :, :, None, :] - splat_positions[None, :, None, :, :]
            gauss = jnp.exp(-0.5 * jnp.sum(diff * diff, -1) / (scales ** 2)[None, :, None, :])
            dirp = jnp.tanh(jnp.einsum('bhsnd,hnd->bhsn', diff, dirn))
            return (gauss, dirp)
        qg, qd = splat_feats(q)
        kg, kd = splat_feats(k)
        amp_b = amps[None, :, None, :]
        splat_attn = jnp.einsum('bhin,bhjn->bhij', amp_b * qg, kg) + directional_strength * jnp.einsum('bhin,bhjn->bhij', amp_b * qg * qd, kg * kd)
        gsa_scores = scores + position_sensitivity * splat_attn
        gsa_out = out_proj(jax.nn.softmax(jnp.where(mask, gsa_scores, neg), axis=-1))
        blend = jnp.minimum(jnp.float32(0.03), jax.nn.sigmoid(gsa_strength) * 0.15)
        return (1.0 - blend) * std_out + blend * gsa_out

    def _L0_ffn_ref(x, w_gate, w_up, w_down):
        import jax, jax.numpy as jnp
        import numpy as np

        def _sparsify_2to4(h):
            B, S, I = h.shape
            g = h.reshape(B, S, I // 4, 4)
            a = jnp.abs(g)
            _, idx = jax.lax.top_k(a, 2)
            pos = jnp.arange(4)
            mask = (pos == idx[..., 0:1]) | (pos == idx[..., 1:2])
            return (g * mask.astype(g.dtype)).reshape(B, S, I)
        h = jax.nn.silu(jnp.einsum('bsh,hi->bsi', x, w_gate)) * jnp.einsum('bsh,hi->bsi', x, w_up)
        h_sparse = _sparsify_2to4(h)
        return jnp.einsum('bsi,ih->bsh', h_sparse, w_down)
    x = L0_attn_hidden_states
    x = _layernorm(x + _L0_attn_ref(x, L0_attn_Wq, L0_attn_Wk, L0_attn_Wv, L0_attn_Wo, L0_attn_splat_positions, L0_attn_splat_directions, L0_attn_splat_log_scales, L0_attn_splat_log_amplitudes, L0_attn_directional_strength, L0_attn_position_sensitivity, L0_attn_gsa_strength), axis=-1)
    x = _layernorm(x + _L0_ffn_ref(x, L0_ffn_w_gate, L0_ffn_w_up, L0_ffn_w_down), axis=-1)
    return x

_drawn_inputs = setup_inputs


def setup_inputs(seed=0):
    import zlib

    import numpy as np

    out = dict(_drawn_inputs(seed))
    spreads = {'L0_attn_splat_log_scales': (-0.2231435477733612, 0.6),
     'L0_attn_splat_log_amplitudes': (-2.079441547393799, 0.6)}
    factors = {'L0_attn_Wq': 8.0,
     'L0_attn_Wk': 8.0,
     'L0_attn_Wv': 3.762,
     'L0_attn_Wo': 3.835,
     'L0_attn_splat_positions': 8.0,
     'L0_attn_splat_directions': 8.0}
    for name, (base, spread) in spreads.items():
        noise = np.random.default_rng([zlib.crc32(name.encode()), seed]).standard_normal(out[name].shape)
        drawn = base * np.exp(spread * noise) if base else spread * noise
        out[name] = jnp.asarray(drawn.astype(out[name].dtype))
    for name, factor in factors.items():
        out[name] = (out[name] * factor).astype(out[name].dtype)
    return out
```

```python
from contextlib import ExitStack

import concourse.bass as bass
from concourse import mybir

F32 = mybir.dt.float32
F32R = mybir.dt.float32r
BF16 = mybir.dt.bfloat16
ALU = mybir.AluOpType
ACT = mybir.ActivationFunctionType
AX = mybir.AxisListType.X

P = 128
BANK = 512
EPS = 1e-5
MASKED = -1e30


def build_kernel(nc, X, WQ, WK, WV, WO, POS, DIR, LSC, LAM, DST, PSE, GSA, WG, WU, WD, OUT):
    _, S, D = X.shape
    H, NS, HD = POS.shape
    I = WG.shape[1]
    T = S // P
    KC = D // P
    PAIRS = H // KC
    HPC = H // KC
    G = S // BANK
    TPG = BANK // P
    SPL = 2 * NS
    assert KC == 2 and SPL == HD and HPC * HD == P and G == 2
    ROWS = 3 * (HD + SPL)
    MROW = ROWS
    SROWS = ROWS + 4
    NB = 3
    NP = 3
    SETS = I // (4 * P)
    HC = I // P
    SCALE = float(HD) ** -0.5

    steps = [(p, g, kt) for p in range(PAIRS) for g in range(G) for kt in range(TPG * (g + 1))]
    SPP = len(steps) // PAIRS

    def q_offset(g, kt):
        return max(0, kt - TPG * g) * P

    def row_items(p):
        return [("max", p, hh, i, c) for hh in range(KC) for i in range(T) for c in range(i // TPG + 1)]

    per_pair = len(row_items(0))
    cost_t = [BANK - min(q_offset(g, kt), BANK // 2) for _, g, kt in steps]
    stream = [it for p in range(PAIRS) for it in row_items(p)]
    cost_m = [BANK if (i // TPG) > c or i % TPG == 3 else P * (i % TPG + 1) for _, _, _, i, c in stream]
    LEAD = 8
    before = stream[:per_pair] + [("turn_max", 0)] + stream[per_pair:per_pair + LEAD]
    at_step = [[] for _ in steps]
    sent = per_pair + LEAD
    total_t, total_m = float(sum(cost_t)), float(sum(cost_m))
    m_start, run_t = float(sum(cost_m[:sent])), 0.0
    run_m = m_start
    pending = []
    for s in range(len(steps)):
        run_t += cost_t[s]
        here = at_step[s]
        while sent < len(stream) and run_m - m_start < run_t * total_m / total_t:
            here.append(stream[sent])
            run_m += cost_m[sent]
            sent += 1
            if sent % per_pair == 0:
                pending.append((s + 1, ("turn_max", sent // per_pair - 1)))
        for at, item in list(pending):
            if at <= s:
                here.append(item)
                pending.remove((at, item))
        p, g, kt = steps[s]
        if g == 1 and kt == 2:
            here.append(("turn_out", p, 0))
        if g == 0 and kt == 3 and p > 0:
            here.append(("turn_out", p - 1, 1))
    assert sent == len(stream) and not pending
    after = [("turn_out", PAIRS - 1, 1)]
    ring = before + [it for here in at_step for it in here] + after
    ring_at = {it: r for r, it in enumerate(ring)}

    with ExitStack() as ctx:
        def sem(name):
            return ctx.enter_context(nc.semaphore(name))

        def sb(name, shape, dt, own=ctx, **kw):
            return own.enter_context(nc.sbuf_tensor(name, shape, dt, **kw))

        ps = ctx.enter_context(nc.psum_tensor("ps", [P, 8, BANK], F32))

        x_sb = sb("x_sb", [P, T, D], F32)
        ident = sb("ident", [P, P], F32)
        ident_bf = sb("ident_bf", [P, P], BF16)
        causal = sb("causal", [P, P], BF16)
        wo_hi = sb("wo_hi", [P, KC, D], F32R)
        wo_lo = sb("wo_lo", [P, KC, D], F32R)
        vx = sb("vx", [P, T, H, 32], F32)
        attn = sb("attn", [P, T, D], F32)
        o_sb = sb("o_sb", [P, 2, BANK], F32)
        mpart = sb("mpart", [P, 2, T, KC, 2], F32)
        mdiff = sb("mdiff", [P, 2, KC, T], F32)
        mrow = sb("mrow", [P, 2, 2, KC, T], F32)
        m_t = sb("m_t", [64, 2, P], F32)
        rec = sb("rec", [P, 16], F32)
        rw = sb("rw", [P, 16], F32)
        otmp = sb("otmp", [P, TPG, KC, 2, HD], F32)
        sc = sb("sc", [P, 8], F32)
        blend = sb("blend", [P, 8, 2], F32)
        par = sb("par", [P, 2 * HD + 2], F32)
        spread_rows = sb("spread_rows", [P, KC, HPC, 2, NS], F32)
        spar = sb("spar", [P, KC, 2 * HD + 2], F32)
        spl = spar[:, :, 0:2 * HD].rearrange("p c (j d) -> p c j d", j=2)
        spk = sb("spk", [P, KC, 16], F32)
        spt = sb("spt", [P, KC, 3, HD], F32)
        spsq = sb("spsq", [P, KC, 2, HD], F32)
        half = sb("half", [P, HPC], F32)
        stats = sb("stats", [P, T, 6], F32)
        mv = sb("mv", [P, T, 2], F32)
        rstd = sb("rstd", [P, T, 3], F32)
        first = ExitStack()
        k_st = [sb("k_st0", [P, KC, S], F32R, first)]
        q_st = [sb("q_st0", [P, KC, S], F32R, first)]
        s_st = [sb("s_st0", [P, KC, S], F32R, first)]

        right = ExitStack()
        base_hi = [sb(f"base_hi{n}", [P, KC, S], F32R, right, side="right") for n in "qk"]
        base_lo = [sb(f"base_lo{n}", [P, KC, S], F32R, right, side="right") for n in "qk"]
        feat_hi = [sb(f"feat_hi{n}", [P, KC, S], F32R, right, side="right") for n in "qk"]
        feat_lo = [sb(f"feat_lo{n}", [P, KC, S], F32R, right, side="right") for n in "qk"]
        right.close()
        wg_hi = sb("wg_hi", [P, KC, SETS, 4, P], F32R, side="right")
        wg_lo = sb("wg_lo", [P, KC, SETS, 4, P], F32R, side="right")
        wu_hi = sb("wu_hi", [P, KC, SETS, 4, P], F32R, side="right")
        wu_lo = sb("wu_lo", [P, KC, SETS, 4, P], F32R, side="right")
        wd_hi = sb("wd_hi", [P, HC, D], F32R, side="right")
        wd_lo = sb("wd_lo", [P, HC, D], F32R, side="right")
        raw = [sb(f"raw{n}", [P, 2 * I], F32, side="right") for n in range(2)]

        early = ExitStack()
        w_nat = sb("w_nat", [P, 4, KC, D], F32, early)
        w_hi = sb("w_hi", [P, 3, KC, D], F32R, early)
        w_lo = sb("w_lo", [P, 3, KC, D], F32R, early)
        xt_hi = sb("xt_hi", [P, KC, S], F32R, early)
        xt_lo = sb("xt_lo", [P, KC, S], F32R, early)
        lin = sb("lin", [P, KC, S], F32, early)
        sq = sb("sq", [P, KC, S], F32, early)
        gauss = sb("gauss", [P, KC, S], F32, early)
        dirp = sb("dirp", [P, KC, S], F32, early)
        xs = attn[:].rearrange("p t d -> p (t d)")[:, 0:KC * 3 * P].rearrange(
            "p (c j h d) -> p c j h d", c=KC, j=3, h=HPC)
        bt = sb("bt", [P, KC, 3, P], F32, early)
        early.close()
        mid = ExitStack()
        for n in range(1, NB):
            k_st.append(sb(f"k_st{n}", [P, KC, S], F32R, mid))
            q_st.append(sb(f"q_st{n}", [P, KC, S], F32R, mid))
            s_st.append(sb(f"s_st{n}", [P, KC, S], F32R, mid))
        pr = sb("pr", [P, NP, 4, BANK], F32, mid)
        mid.close()
        first.close()
        y = attn
        yt_hi = sb("yt_hi", [P, KC, S], F32R)
        yt_lo = sb("yt_lo", [P, KC, S], F32R)
        tail = ExitStack()
        at_hi = sb("at_hi", [P, KC, S], F32R, tail)
        at_lo = sb("at_lo", [P, KC, S], F32R, tail)
        tail.close()
        ht_hi = sb("ht_hi", [P, HC, BANK], F32R)
        ht_lo = sb("ht_lo", [P, HC, BANK], F32R)
        sg = sb("sg", [P, 2, BANK], F32)
        hid = sb("hid", [P, 2, 4, BANK], F32)
        mag = sb("mag", [P, 4, BANK], F32)
        beats = sb("beats", [P, 6, BANK], BF16)
        sums = sb("sums", [P, 4, BANK], BF16)
        wins = sb("wins", [P, 4, BANK], BF16)

        x_loaded, w_loaded, spl_loaded = sem("x_loaded"), sem("w_loaded"), sem("spl_loaded")
        consts = sem("consts")
        ident_cast = sem("ident_cast")
        spl_act, spl_dve = sem("spl_act"), sem("spl_dve")
        spread, by_row = sem("spread"), sem("by_row")
        a_pe, a_act, a_dve = sem("a_pe"), sem("a_act"), sem("a_dve")
        lin_read = sem("lin_read")
        feat_f, feat_h, feat_l = sem("feat_f"), sem("feat_h"), sem("feat_l")
        attn_done = sem("attn_done")
        reused = sem("reused")
        st_loaded = [sem(f"st_loaded{b}") for b in range(NB)]
        m_loaded = sem("m_loaded")
        ring_full, ring_free = sem("ring_full"), sem("ring_free")
        rows_ready = sem("rows_ready")
        s_full, exp_done = sem("s_full"), sem("exp_done")
        pattn_done, o_evac = sem("pattn_done"), sem("o_evac")
        chain = sem("chain")
        raw_loaded = [sem(f"raw_loaded{n}") for n in range(3)]
        prep = sem("prep")
        f_pe, f_act, f_dve = sem("f_pe"), sem("f_act"), sem("f_dve")
        var_ready, std_ready, y_ready = sem("var_ready"), sem("std_ready"), sem("y_ready")
        mag_ready = sem("mag_ready")
        sparse_ready, sparse_hi, sparse_lo = sem("sparse_ready"), sem("sparse_hi"), sem("sparse_lo")
        out_ready, stored = sem("out_ready"), sem("stored")

        A_USES = ([("xt", b) for b in range(4)] + [("wt", 0), ("wt", 1), ("bt", 0), ("bt", 1)]
                  + [("proj", 0, hf, c) for hf in range(2) for c in range(2)] + [("wt", 2)]
                  + [(k, 0, hf, c) for hf in range(2) for c in range(2) for k in ("gauss", "dirp")]
                  + [("proj", 1, hf, c) for hf in range(2) for c in range(2)]
                  + [("v", 0), ("v", 1)]
                  + [(k, 1, hf, c) for hf in range(2) for c in range(2) for k in ("gauss", "dirp")]
                  + [("v", 2), ("v", 3), ("wt", 3)])
        A_READ = {"xt": "ad", "wt": "ad", "bt": "d", "proj": "ad", "gauss": "a", "dirp": "a", "v": "a"}
        F_USES = ([("at", b) for b in range(4)] + [("wo", b) for b in range(4)] + [("yt", b) for b in range(4)]
                  + [(k, 0, s, c) for s in range(SETS) for c in range(4) for k in ("gate", "up")]
                  + [(k, 1, 0, c) for c in range(4) for k in ("gate", "up")]
                  + [("down", 0), ("down", 1)]
                  + [(k, 1, s, c) for s in range(1, SETS) for c in range(4) for k in ("gate", "up")]
                  + [("down", 2), ("down", 3)])
        F_READ = {"at": "ad", "wo": "d", "yt": "ad", "gate": "a", "up": "d", "down": "d"}

        def counted(uses, read, who):
            out = [0]
            for u in uses:
                out.append(out[-1] + (who in read[u[0]]))
            return out

        A_ACT, A_DVE = counted(A_USES, A_READ, "a"), counted(A_USES, A_READ, "d")
        F_ACT, F_DVE = counted(F_USES, F_READ, "a"), counted(F_USES, F_READ, "d")
        a_index = {u: n for n, u in enumerate(A_USES)}
        f_index = {u: n for n, u in enumerate(F_USES)}

        def hidden_count(m):
            return F_DVE[f_index[("up", m // (4 * SETS), m // 4 % SETS, m % 4)] + 1]

        def bank_free(pe, uses, read, acts, dves, act_sem, dve_sem, n):
            if n >= 8:
                if "a" in read[uses[n - 8][0]]:
                    pe.wait_ge(act_sem, acts[n - 7])
                if "d" in read[uses[n - 8][0]]:
                    pe.wait_ge(dve_sem, dves[n - 7])

        block = ctx.enter_context(nc.Block())

        @block.sync
        def _(sp):
            xv = X[0].rearrange("(t p) d -> p t d", p=P)
            sp.dma_start(x_sb[:, 0:4, :], xv[:, 0:4, :]).then_inc(x_loaded, 16)
            sp.dma_start(x_sb[:, 4:8, :], xv[:, 4:8, :]).then_inc(x_loaded, 16)

            def stack(p):
                b, r = p % NB, HD * p
                parts = ((q_st[b], base_hi[0], 0), (q_st[b], base_hi[0], 1), (q_st[b], base_lo[0], 2),
                         (q_st[b], feat_hi[0], 3), (q_st[b], feat_hi[0], 4), (q_st[b], feat_lo[0], 5),
                         (k_st[b], base_hi[1], 0), (k_st[b], base_lo[1], 1), (k_st[b], base_hi[1], 2),
                         (k_st[b], feat_hi[1], 3), (k_st[b], feat_lo[1], 4), (k_st[b], feat_hi[1], 5),
                         (s_st[b], base_hi[0], 0), (s_st[b], base_hi[0], 1), (s_st[b], base_lo[0], 2))
                for dst, src, n in parts:
                    sp.dma_start(dst[HD * n:HD * n + HD, :, :].bitcast(F32),
                                 src[r:r + HD, :, :].bitcast(F32)).then_inc(st_loaded[b], 16)

            def maxima(p):
                sp.wait_ge(ring_free, ring_at[("turn_max", p)] + 1)
                b = p % NB
                sp.dma_start(q_st[b][MROW:MROW + 4, :, :].bitcast(F32), m_t[0:64, p % 2, :]).then_inc(m_loaded, 16)
                sp.dma_start(s_st[b][MROW:MROW + 2, :, :].bitcast(F32), m_t[0:32, p % 2, :]).then_inc(m_loaded, 16)

            sp.wait_ge(consts, 6)
            sp.wait_ge(a_act, A_ACT[a_index[("proj", 1, 1, 1)] + 1])
            sp.wait_ge(a_dve, A_DVE[a_index[("proj", 1, 1, 1)] + 1])
            sp.wait_ge(feat_h, 8)
            sp.wait_ge(feat_l, 8)
            stack(0)
            sp.wait_ge(reused, 2 * (NB - 1))
            stack(1)
            stack(2)
            maxima(0)
            for p in range(PAIRS):
                if p + 1 < PAIRS:
                    maxima(p + 1)
                if p + 3 < PAIRS:
                    sp.wait_ge(s_full, 4 * SPP * (p + 1))
                    stack(p + 3)
                if p + 3 == PAIRS - 1:
                    for b in range(NB):
                        sp.wait_ge(st_loaded[b], 16 * 15 * len(range(b, PAIRS, NB)))
                    sp.dma_start(raw[0][:], WG.rearrange("(k p) i -> p k i", p=P)).then_inc(raw_loaded[0], 16)
                    sp.dma_start(raw[1][:], WU.rearrange("(k p) i -> p k i", p=P)).then_inc(raw_loaded[1], 16)
            sp.wait_ge(prep, 8)
            sp.dma_start(raw[0][:], WD.rearrange("(s j c) n -> j s c n", s=SETS, c=4)).then_inc(raw_loaded[2], 16)
            ov = OUT[0].rearrange("(t p) d -> p t d", p=P)
            for t in range(T):
                sp.wait_ge(out_ready, t + 1)
                sp.dma_start(ov[:, t, :], x_sb[:, t, :]).then_inc(stored, 16)
            sp.wait_ge(stored, 16 * T)

        @block.gpsimd
        def _(pool):
            pool.memset(ident[:], 0.0).then_inc(consts, 1)
            pool.memset(causal[:], 0.0).then_inc(consts, 1)
            pool.wait_ge(consts, 2)
            pool.affine_select(out=ident[:], in_=ident[:], compare_op=ALU.not_equal, fill=1.0, base=0,
                               pattern=[[-1, P]], channel_multiplier=1).then_inc(consts, 1)
            pool.affine_select(out=causal[:], in_=causal[:], compare_op=ALU.is_ge, fill=MASKED, base=0,
                               pattern=[[-1, P]], channel_multiplier=1).then_inc(consts, 1)
            pool.memset(spread_rows[:], 0.0).then_inc(spread, 1)
            pool.wait_ge(spread, 1)
            for c in range(KC):
                pool.affine_select(out=spread_rows[:, c], in_=spread_rows[:, c], compare_op=ALU.not_equal, fill=1.0,
                                   base=-HPC * NS * c, pattern=[[-NS, HPC], [0, 2], [-1, NS]],
                                   channel_multiplier=1).then_inc(spread, 1)
            pool.memset(s_st[0][:].bitcast(F32), 0.0).then_inc(consts, 1)
            pool.wait_ge(consts, 5)
            pool.memset(k_st[0][ROWS:SROWS].bitcast(F32), 1.0).then_inc(consts, 1)
            pool.wait_ge(consts, 6)
            pool.memset(half[:], 1.0).then_inc(consts, 1)
            pool.wait_ge(consts, 7)
            pool.affine_select(out=half[:], in_=half[:], compare_op=ALU.is_ge, fill=0.0, base=-NS,
                               pattern=[[-HD, HPC]], channel_multiplier=1).then_inc(consts, 1)
            pool.wait_ge(consts, 8)
            pool.affine_select(out=half[:], in_=half[:], compare_op=ALU.is_ge, fill=0.0, base=HD - 1,
                               pattern=[[HD, HPC]], channel_multiplier=-1).then_inc(consts, 1)
            pool.memset(vx[:, :, :, HD:32], 1.0).then_inc(consts, 1)
            pool.wait_ge(spread, 4)
            blocks = xs.rearrange("p c j h d -> p (c j) h d")
            pool.affine_select(out=blocks, in_=blocks, compare_op=ALU.is_ge, fill=0.0, base=0,
                               pattern=[[0, 6], [-HD, HPC], [0, HD]], channel_multiplier=1).then_inc(spread, 1)
            pool.wait_ge(spread, 5)
            pool.affine_select(out=blocks, in_=blocks, compare_op=ALU.is_ge, fill=0.0, base=HD - 1,
                               pattern=[[0, 6], [HD, HPC], [0, HD]], channel_multiplier=-1).then_inc(spread, 1)
            for n in range(8):
                w, hf, c = n // 4, n // 2 % 2, n % 2
                cols = slice(hf * BANK, hf * BANK + BANK)
                pool.wait_ge(feat_h, n + 1)
                pool.tensor_tensor(feat_lo[w][:, c, cols], gauss[:, c, cols], feat_hi[w][:, c, cols].bitcast(F32),
                                   ALU.subtract).then_inc(feat_l, 1)
            pool.wait_ge(a_pe, len(A_USES))
            pool.wait_ge(a_act, A_ACT[-1])
            pool.wait_ge(a_dve, A_DVE[-1])
            pool.wait_ge(feat_l, 8)
            for b in range(1, NB):
                pool.memset(s_st[b][:].bitcast(F32), 0.0).then_inc(reused, 1)
                pool.wait_ge(reused, 2 * b - 1)
                pool.memset(k_st[b][ROWS:SROWS].bitcast(F32), 1.0).then_inc(reused, 1)
                pool.wait_ge(reused, 2 * b)

            def slices():
                for n, (src, hi, lo) in enumerate(((raw[0], wg_hi, wg_lo), (raw[1], wu_hi, wu_lo))):
                    rv = src[:].rearrange("p (k s j c) -> p k s c j", k=KC, s=SETS, c=4)
                    for k in range(KC):
                        for s in range(SETS):
                            yield n, rv[:, k, s], hi[:, k, s], lo[:, k, s]
                rv = raw[0][:].rearrange("p (m n) -> p m n", m=HC)
                for m in range(0, HC, 2):
                    yield 2, rv[:, m:m + 2], wd_hi[:, m:m + 2], wd_lo[:, m:m + 2]

            for m, (n, src, hi, lo) in enumerate(slices()):
                pool.wait_ge(raw_loaded[n], 16)
                pool.tensor_scalar(hi, src, 1.0, 0.0, ALU.mult, ALU.add).then_inc(prep, 1)
                pool.wait_ge(prep, 2 * m + 1)
                pool.tensor_tensor(lo, src, hi.bitcast(F32), ALU.subtract).then_inc(prep, 1)
            for n in range(2):
                for s in range(SETS):
                    u = n * SETS + s
                    for c in range(4):
                        pool.wait_ge(sparse_hi, 4 * u + c + 1)
                        pool.tensor_tensor(ht_lo[:, 4 * s + c, :], hid[:, u % 2, c, :],
                                           ht_hi[:, 4 * s + c, :].bitcast(F32), ALU.subtract).then_inc(sparse_lo, 1)

        def magnitude(act, m):
            u, c = m // 4, m % 4
            act.wait_ge(f_dve, hidden_count(m))
            if c == 0 and u >= 1:
                act.wait_ge(sparse_ready, 4 * u)
            act.activation(mag[:, c, :], hid[:, u % 2, c, :], ACT.Abs).then_inc(mag_ready, 1)

        def highs(act, u):
            n, s = u // SETS, u % SETS
            if n >= 1 and s == 0:
                act.wait_ge(f_pe, f_index[("down", 1)] + 1)
            for c in range(4):
                act.wait_ge(sparse_ready, 4 * u + c + 1)
                act.activation(ht_hi[:, 4 * s + c, :], hid[:, u % 2, c, :], ACT.Copy).then_inc(sparse_hi, 1)

        @block.scalar
        def _(act):
            for n, w in enumerate((WQ, WK, WV, WO)):
                act.dma_start(w_nat[:, n], w.rearrange("(c p) d -> p c d", p=P)).then_inc(w_loaded, 16)
            for v, cols in ((POS, slice(0, HD)), (DIR, slice(HD, 2 * HD))):
                act.dma_start(par[:, cols], v.rearrange("h n d -> (h n) d")).then_inc(spl_loaded, 16)
            for v, col in ((LSC, 2 * HD), (LAM, 2 * HD + 1)):
                act.dma_start(par[:, col:col + 1], v.rearrange("h (n o) -> (h n) o", o=1)).then_inc(spl_loaded, 16)
            for j, v in enumerate((DST, PSE, GSA)):
                act.dma_start(sc[:, j:j + 1], bass.AP(tensor=v.tensor, offset=0, ap=[[0, P], [1, 1]])).then_inc(spl_loaded, 16)
            act.wait_ge(spl_loaded, 16 * 7)
            act.wait_ge(spl_dve, 1)
            act.activation(spk[:, :, 2:3], spar[:, :, 2 * HD:2 * HD + 1], ACT.Exp, scale=-2.0)
            act.activation(spk[:, :, 3:4], spar[:, :, 2 * HD + 1:2 * HD + 2], ACT.Exp)
            act.activation(sc[:, 3:4], sc[:, 2:3], ACT.Exp, scale=-1.0).then_inc(spl_act, 1)
            act.wait_ge(spl_dve, 2)
            act.activation(spk[:, :, 5:6], spk[:, :, 4:5], ACT.Sqrt).then_inc(spl_act, 1)

            n_feat = 0
            for n, use in enumerate(A_USES):
                kind, bank = use[0], n % 8
                if "a" not in A_READ[kind]:
                    continue
                act.wait_ge(a_pe, n + 1)
                if kind == "xt":
                    b = use[1]
                    act.activation(xt_hi[:, :, 2 * P * b:2 * P * (b + 1)],
                                   ps[:, bank, :].rearrange("p (k t) -> p k t", k=KC), ACT.Copy).then_inc(a_act, 1)
                elif kind == "wt":
                    w = use[1]
                    dst = w_hi[:, w] if w < 3 else wo_hi[:]
                    act.activation(dst, ps[:, bank, :].rearrange("p (k t) -> p k t", k=KC), ACT.Copy).then_inc(a_act, 1)
                elif kind == "proj":
                    _, w, hf, c = use
                    cols = slice(hf * BANK, hf * BANK + BANK)
                    act.activation(base_hi[w][:, c, cols], ps[:, bank, :], ACT.Copy, scale=SCALE if w == 0 else 1.0)
                    if w == 1:
                        act.wait_ge(a_pe, a_index[("gauss", 0, hf, c)] + 1)
                    act.activation(sq[:, c, cols], ps[:, bank, :], ACT.Square).then_inc(a_act, 1)
                elif kind in ("gauss", "dirp"):
                    _, w, hf, c = use
                    cols = slice(hf * BANK, hf * BANK + BANK)
                    if kind == "gauss":
                        act.wait_ge(spl_dve, 3)
                        if w == 1:
                            act.wait_ge(feat_l, n_feat - 4 + 1)
                        act.activation(gauss[:, c, cols], ps[:, bank, :], ACT.Exp,
                                       bias=spk[:, c, 6:7]).then_inc(a_act, 1)
                    else:
                        if w == 1:
                            act.wait_ge(feat_f, n_feat - 4 + 1)
                        act.activation(dirp[:, c, cols], ps[:, bank, :], ACT.Tanh,
                                       bias=spk[:, c, 7:8]).then_inc(a_act, 1)
                        n_feat += 1
                        if n_feat % 4 != 1:
                            m = n_feat - 2
                            act.wait_ge(feat_f, m + 1)
                            mc = slice(m // 2 % 2 * BANK, (m // 2 % 2 + 1) * BANK)
                            act.activation(feat_hi[m // 4][:, m % 2, mc], gauss[:, m % 2, mc], ACT.Copy).then_inc(feat_h, 1)
                        if n_feat in (4, 8):
                            m = n_feat - 1
                            act.wait_ge(feat_f, m + 1)
                            mc = slice(m // 2 % 2 * BANK, (m // 2 % 2 + 1) * BANK)
                            act.activation(feat_hi[m // 4][:, m % 2, mc], gauss[:, m % 2, mc], ACT.Copy).then_inc(feat_h, 1)
                elif kind == "v":
                    t = 2 * use[1]
                    act.wait_ge(consts, 10)
                    act.activation(vx[:, t:t + 2, :, 0:HD],
                                   ps[:, bank, :].rearrange("p (t h d) -> p t h d", t=2, h=H), ACT.Copy).then_inc(a_act, 1)

            def evacuate(n):
                last = SPP * (n // G) + (TPG if n % G == 0 else SPP)
                act.wait_ge(pattn_done, last)
                if n >= 2:
                    act.wait_ge(ring_full, ring_at[("turn_out", (n - 2) // G, n % G)] + 1)
                act.activation(o_sb[:, n % 2, :], ps[:, 7, :], ACT.Copy).then_inc(o_evac, 1)

            act.wait_ge(reused, 2 * (NB - 1))
            for s, (p, g, kt) in enumerate(steps):
                off = q_offset(g, kt)
                for t in range(4):
                    n = 4 * s + t
                    act.wait_ge(s_full, n + 1)
                    if s >= NP and t == 0:
                        act.wait_ge(pattn_done, s - NP + 1)
                    act.activation(pr[:, s % NP, t, off:BANK], ps[:, 4 + n % 3, off:BANK], ACT.Exp).then_inc(exp_done, 1)
                if kt == 0 and s > 0:
                    evacuate(G * p + g - 1)
            evacuate(G * PAIRS - 1)

            n_std = 0
            for n, use in enumerate(F_USES):
                kind, bank = use[0], n % 8
                if kind == "yt" and n_std == 0:
                    for hf in range(2):
                        act.wait_ge(var_ready, hf + 1)
                        act.activation(rstd[:, 4 * hf:4 * hf + 4, 1:2], rstd[:, 4 * hf:4 * hf + 4, 0:1],
                                       ACT.Sqrt).then_inc(std_ready, 1)
                    n_std = 2
                if "a" not in F_READ[kind]:
                    continue
                act.wait_ge(f_pe, n + 1)
                if kind in ("at", "yt"):
                    b = use[1]
                    dst = at_hi if kind == "at" else yt_hi
                    act.activation(dst[:, :, 2 * P * b:2 * P * (b + 1)],
                                   ps[:, bank, :].rearrange("p (k t) -> p k t", k=KC), ACT.Copy).then_inc(f_act, 1)
                elif kind == "gate":
                    _, nn, s, c = use
                    u = nn * SETS + s
                    m = 4 * u + c
                    if m >= 2:
                        act.wait_ge(f_dve, hidden_count(m - 2))
                    act.activation(sg[:, m % 2, :], ps[:, bank, :], ACT.Silu).then_inc(f_act, 1)
                    if m >= 1:
                        magnitude(act, m - 1)
                    if c == 2 and u >= 1:
                        highs(act, u - 1)
            magnitude(act, 8 * SETS - 1)
            highs(act, 2 * SETS - 1)
            for hf in range(2):
                act.wait_ge(var_ready, 3 + hf)
                act.activation(rstd[:, 4 * hf:4 * hf + 4, 1:2], rstd[:, 4 * hf:4 * hf + 4, 0:1],
                               ACT.Sqrt).then_inc(std_ready, 1)

        @block.tensor
        def _(pe):
            def three(out, lhs, rhs, first, last, **kw):
                pe.matmul(out, lhs[0], rhs[0], start=first, stop=False, **kw)
                pe.matmul(out, lhs[0], rhs[1], start=False, stop=False, **kw)
                return pe.matmul(out, lhs[1], rhs[0], start=False, stop=last, **kw)

            pe.wait_ge(consts, 4)
            for n, use in enumerate(A_USES):
                kind, bank = use[0], n % 8
                bank_free(pe, A_USES, A_READ, A_ACT, A_DVE, a_act, a_dve, n)
                if n == 4:
                    pe.wait_ge(spl_loaded, 16 * 7)
                    pe.wait_ge(spread, 3)
                    for c in range(KC):
                        mm = pe.matmul(ps[:, 7, c * (2 * HD + 2):(c + 1) * (2 * HD + 2)],
                                       spread_rows[:, c].rearrange("p h f n -> p (h f n)"), par[:], start=True, stop=True)
                    mm.then_inc(by_row, 1)
                if kind == "xt":
                    b = use[1]
                    pe.wait_ge(x_loaded, 32)
                    for k in range(KC):
                        for t in range(2):
                            o = (2 * k + t) * P
                            mm = pe.transpose(ps[:, bank, o:o + P], x_sb[:, 2 * b + t, P * k:P * (k + 1)], ident[:])
                elif kind == "wt":
                    w = use[1]
                    pe.wait_ge(w_loaded, 64)
                    for k in range(KC):
                        for c in range(KC):
                            o = (2 * k + c) * P
                            mm = pe.transpose(ps[:, bank, o:o + P], w_nat[:, w, c, P * k:P * (k + 1)], ident[:])
                elif kind == "bt":
                    c = use[1]
                    pe.wait_ge(spread, 6)
                    for j in range(3):
                        mm = pe.transpose(ps[:, bank, j * P:(j + 1) * P],
                                          xs[:, c, j].rearrange("p h d -> p (h d)"), ident[:])
                elif kind == "proj":
                    _, w, hf, c = use
                    cols = slice(hf * BANK, hf * BANK + BANK)
                    dims = slice(P * c, P * c + P)
                    pe.wait_ge(a_dve, A_DVE[a_index[("wt", w)] + 1])
                    for k in range(KC):
                        mm = three(ps[:, bank, :], (w_hi[:, w, k, dims], w_lo[:, w, k, dims]),
                                   (xt_hi[:, k, cols], xt_lo[:, k, cols]), k == 0, k == KC - 1)
                elif kind == "gauss":
                    _, w, hf, c = use
                    cols = slice(hf * BANK, hf * BANK + BANK)
                    pe.wait_ge(a_dve, A_DVE[a_index[("proj", w, hf, c)] + 1])
                    pe.wait_ge(a_dve, A_DVE[a_index[("bt", 1)] + 1])
                    pe.matmul(ps[:, bank, :], bt[:, c, 0], lin[:, c, cols], start=True, stop=False)
                    mm = pe.matmul(ps[:, bank, :], bt[:, c, 2], sq[:, c, cols], start=False, stop=True)
                elif kind == "dirp":
                    _, w, hf, c = use
                    mm = pe.matmul(ps[:, bank, :], bt[:, c, 1], lin[:, c, hf * BANK:hf * BANK + BANK],
                                   start=True, stop=True)
                elif kind == "v":
                    pe.wait_ge(a_dve, A_DVE[a_index[("wt", 2)] + 1])
                    for j in range(2):
                        t = 2 * use[1] + j
                        tok = slice(P * t, P * t + P)
                        for k in range(KC):
                            mm = three(ps[:, bank, j * D:(j + 1) * D], (xt_hi[:, k, tok], xt_lo[:, k, tok]),
                                       (w_hi[:, 2, k, :], w_lo[:, 2, k, :]), k == 0, k == KC - 1)
                mm.then_inc(a_pe, 1)
            pe.wait_ge(a_act, A_ACT[-1])
            pe.wait_ge(a_dve, A_DVE[-1])
            pe.wait_ge(ident_cast, 1)

            def item(it):
                r = ring_at[it]
                slot = 2 * (r % 2)
                if r >= 2:
                    pe.wait_ge(ring_free, r - 1)
                if it[0] == "max":
                    _, p, hh, i, c = it
                    b = p % NB
                    if hh == 0 and i == 0:
                        pe.wait_ge(st_loaded[b], 16 * 15 * (p // NB + 1))
                    lo = BANK * c
                    n = min(BANK, (i + 1) * P - lo)
                    wide = max(n, 2 * P)
                    for v, st in enumerate((s_st[b], q_st[b])):
                        mm = pe.matmul(ps[:, slot + v, 0:wide], st[0:ROWS, hh, i * P:(i + 1) * P],
                                       k_st[b][0:ROWS, hh, lo:lo + wide], start=True, stop=True)
                        if c == i // TPG:
                            mm = pe.matmul(ps[:, slot + v, n - P:n], ident_bf[:], causal[:],
                                           start=False, stop=True, skip_group_check=True)
                elif it[0] == "turn_max":
                    p = it[1]
                    pe.wait_ge(rows_ready, p + 1)
                    mm = pe.transpose(ps[0:64, slot, 0:P], mrow[:].rearrange("p a b h t -> p (a b h t)"), ident[:])
                else:
                    _, p, g = it
                    n = G * p + g
                    pe.wait_ge(o_evac, n + 1)
                    for t in range(TPG):
                        mm = pe.transpose(ps[:, slot, t * P:(t + 1) * P], o_sb[:, n % 2, t * P:(t + 1) * P], ident[:])
                mm.then_inc(ring_full, 1)

            def values(s):
                p, g, kt = steps[s]
                off = q_offset(g, kt)
                pe.wait_ge(exp_done, 4 * s + 4)
                if kt == 0 and s > 0:
                    pe.wait_ge(o_evac, G * p + g)
                for t in range(4):
                    mm = pe.matmul(ps[32 * t:32 * t + 32, 7, off:BANK], vx[:, kt, p + HPC * (t // 2), :],
                                   pr[:, s % NP, t, off:BANK], start=(kt == 0), stop=(kt == TPG * (g + 1) - 1),
                                   skip_group_check=True)
                mm.then_inc(pattn_done, 1)

            for it in before:
                item(it)
            for s, (p, g, kt) in enumerate(steps):
                b = p % NB
                if g == 0 and kt == 0:
                    pe.wait_ge(m_loaded, 32 * (p + 1))
                off = min(q_offset(g, kt), BANK // 2)
                mine = list(at_step[s])
                for t in range(4):
                    n = 4 * s + t
                    if n >= 3:
                        pe.wait_ge(exp_done, n - 2)
                    st = (s_st[b], q_st[b])[t % 2]
                    mm = pe.matmul(ps[:, 4 + n % 3, off:BANK], k_st[b][0:SROWS, t // 2, kt * P:(kt + 1) * P],
                                   st[0:SROWS, t // 2, g * BANK + off:(g + 1) * BANK], start=True, stop=True)
                    if kt >= TPG * g:
                        diagonal = q_offset(g, kt)
                        mm = pe.matmul(ps[:, 4 + n % 3, diagonal:diagonal + P], causal[:], ident_bf[:],
                                       start=False, stop=True, skip_group_check=True)
                    mm.then_inc(s_full, 1)
                    if t % 2 == 1 and mine:
                        item(mine.pop(0))
                for it in mine:
                    item(it)
                if s >= 1:
                    values(s - 1)
            values(len(steps) - 1)
            for it in after:
                item(it)

            pe.wait_ge(exp_done, 4 * len(steps))
            pe.wait_ge(o_evac, G * PAIRS)
            pe.wait_ge(ring_free, len(ring))
            pe.wait_ge(attn_done, G * PAIRS)
            for n, use in enumerate(F_USES):
                kind, bank = use[0], n % 8
                bank_free(pe, F_USES, F_READ, F_ACT, F_DVE, f_act, f_dve, n)
                if kind in ("at", "yt"):
                    b = use[1]
                    src = attn if kind == "at" else y
                    if kind == "yt":
                        pe.wait_ge(y_ready, 2 * b + 2)
                    for k in range(KC):
                        for t in range(2):
                            o = (2 * k + t) * P
                            mm = pe.transpose(ps[:, bank, o:o + P], src[:, 2 * b + t, P * k:P * (k + 1)], ident[:])
                elif kind == "wo":
                    b = use[1]
                    pe.wait_ge(f_dve, F_DVE[f_index[("at", b)] + 1])
                    for j in range(2):
                        tok = slice(P * (2 * b + j), P * (2 * b + j + 1))
                        for k in range(KC):
                            mm = three(ps[:, bank, j * D:(j + 1) * D], (at_hi[:, k, tok], at_lo[:, k, tok]),
                                       (wo_hi[:, k, :], wo_lo[:, k, :]), k == 0, k == KC - 1)
                elif kind in ("gate", "up"):
                    _, nn, s, c = use
                    cols = slice(nn * BANK, nn * BANK + BANK)
                    pe.wait_ge(f_dve, F_DVE[f_index[("yt", 2 * nn + 1)] + 1])
                    if n == f_index[("gate", 0, 0, 0)]:
                        pe.wait_ge(prep, 24)
                    hi, lo = (wg_hi, wg_lo) if kind == "gate" else (wu_hi, wu_lo)
                    for k in range(KC):
                        mm = three(ps[:, bank, :], (hi[:, k, s, c], lo[:, k, s, c]),
                                   (yt_hi[:, k, cols], yt_lo[:, k, cols]), k == 0, k == KC - 1)
                else:
                    b = use[1]
                    pe.wait_ge(sparse_lo, 4 * SETS * (b // 2 + 1))
                    for j in range(2):
                        tok = slice(P * (2 * (b % 2) + j), P * (2 * (b % 2) + j + 1))
                        for m in range(HC):
                            mm = three(ps[:, bank, j * D:(j + 1) * D], (ht_hi[:, m, tok], ht_lo[:, m, tok]),
                                       (wd_hi[:, m, :], wd_lo[:, m, :]), m == 0, m == HC - 1)
                mm.then_inc(f_pe, 1)

        def sparsify(dve, link, u):
            h = hid[:, u % 2]
            dve.wait_ge(mag_ready, 4 * u + 4)
            dve.tensor_tensor(beats[:, 0:3, :], mag[:, 0:1, :].broadcast_to([P, 3, BANK]), mag[:, 1:4, :], ALU.is_ge)
            dve.tensor_tensor(beats[:, 3:5, :], mag[:, 1:2, :].broadcast_to([P, 2, BANK]), mag[:, 2:4, :], ALU.is_ge)
            link(dve.tensor_tensor(beats[:, 5, :], mag[:, 2, :], mag[:, 3, :], ALU.is_ge))
            dve.tensor_tensor(sums[:, 0:2, :], beats[:, 0:4:3, :], beats[:, 1:5:3, :], ALU.add)
            link(dve.tensor_tensor(sums[:, 2:4, :], beats[:, 1:3, :], beats[:, 3:5, :], ALU.add))
            dve.tensor_tensor(wins[:, 0:4:3, :], sums[:, 0:4:3, :], beats[:, 2:6:3, :], ALU.add)
            link(dve.tensor_tensor(wins[:, 1:3, :], sums[:, 1:3, :], beats[:, 0:6:5, :], ALU.subtract))
            for c, (limit, op) in enumerate(((2.0, ALU.is_ge), (1.0, ALU.is_ge), (0.0, ALU.is_le), (1.0, ALU.is_le))):
                dve.scalar_tensor_tensor(out=h[:, c, :], in0=wins[:, c, :], scalar=limit, in1=h[:, c, :],
                                         op0=op, op1=ALU.mult).then_inc(sparse_ready, 1)

        @block.vector
        def _(dve):
            links = [0]

            def link(ins):
                links[0] += 1
                ins.then_inc(chain, 1)
                dve.wait_ge(chain, links[0])

            dve.wait_ge(consts, 4)
            dve.tensor_copy(ident_bf[:], ident[:]).then_inc(ident_cast, 1)
            dve.wait_ge(spl_loaded, 16 * 7)
            dve.wait_ge(by_row, 1)
            dve.tensor_copy(spar[:], ps[:, 7, 0:KC * (2 * HD + 2)].rearrange("p (c e) -> p c e", c=KC)).then_inc(spl_dve, 1)
            dve.wait_ge(spl_dve, 1)
            dve.tensor_tensor(spsq[:, :, 1, :], spl[:, :, 1, :], spl[:, :, 1, :], ALU.mult)
            link(dve.tensor_tensor(spsq[:, :, 0, :], spl[:, :, 0, :], spl[:, :, 0, :], ALU.mult))
            dve.wait_ge(spl_act, 1)
            dve.tensor_reduce(spk[:, :, 8:9], spsq[:, :, 0, :], AX, ALU.add)
            dve.tensor_reduce(spk[:, :, 4:5], spsq[:, :, 1, :], AX, ALU.add).then_inc(spl_dve, 1)
            link(dve.tensor_scalar(sc[:, 4:5], sc[:, 3:4], 1.0, None, ALU.add))
            link(dve.reciprocal(sc[:, 5:6], sc[:, 4:5]))
            link(dve.tensor_scalar(sc[:, 6:7], sc[:, 5:6], 0.15, 0.03, ALU.mult, ALU.min))
            dve.tensor_copy(blend[:, :, 1:2], sc[:, 6:7].unsqueeze(1).broadcast_to([P, 8, 1]))
            dve.tensor_scalar(blend[:, :, 0:1], sc[:, 6:7].unsqueeze(1).broadcast_to([P, 8, 1]), -1.0, 1.0, ALU.mult, ALU.add)
            dve.wait_ge(consts, 9)
            link(dve.tensor_reduce(spk[:, 0, 9:10], half[:], AX, ALU.add))
            dve.tensor_copy(spk[:, 1, 9:10], spk[:, 0, 9:10])
            dve.tensor_scalar(spk[:, :, 10:11], spk[:, 0, 9:10].unsqueeze(1).broadcast_to([P, KC, 1]), -1.0, 1.0, ALU.mult, ALU.add)
            dve.tensor_scalar(spk[:, :, 11:12], spk[:, 0, 9:10].unsqueeze(1).broadcast_to([P, KC, 1]), sc[:, 0:1], None, ALU.mult)
            dve.tensor_scalar(spk[:, :, 12:13], spk[:, :, 3:4], sc[:, 1:2], None, ALU.mult)
            link(dve.tensor_scalar(spk[:, :, 13:14], spk[:, :, 2:3], -0.5, None, ALU.mult))
            dve.wait_ge(spl_act, 2)
            link(dve.tensor_scalar(spk[:, :, 14:15], spk[:, :, 5:6], 1e-8, None, ALU.add))
            link(dve.reciprocal(spk[:, :, 15:16], spk[:, :, 14:15]))
            dve.tensor_tensor(spt[:, :, 0, :], spl[:, :, 0, :], spk[:, :, 2:3].broadcast_to([P, KC, HD]), ALU.mult)
            dve.tensor_tensor(spt[:, :, 2, :], spk[:, :, 13:14].broadcast_to([P, KC, HD]),
                              half[:, 0:1].unsqueeze(1).broadcast_to([P, KC, HD]), ALU.bypass)
            link(dve.tensor_tensor(spt[:, :, 1, :], spl[:, :, 1, :], spk[:, :, 15:16].broadcast_to([P, KC, HD]), ALU.mult))
            dve.tensor_tensor(spk[:, :, 6:7], spk[:, :, 8:9], spk[:, :, 13:14], ALU.mult)
            link(dve.tensor_tensor(spsq[:, :, 0, :], spl[:, :, 0, :], spt[:, :, 1, :], ALU.mult))
            link(dve.tensor_reduce(spk[:, :, 4:5], spsq[:, :, 0, :], AX, ALU.add))
            dve.tensor_scalar(spk[:, :, 7:8], spk[:, :, 4:5], -1.0, None, ALU.mult).then_inc(spl_dve, 1)
            for c in range(KC):
                ins = dve.tensor_copy(xs[:, c], spt[:, c].unsqueeze(2).broadcast_to([P, 3, HPC, HD]))
            ins.then_inc(spread, 1)

            n_feat = 0
            for n, use in enumerate(A_USES):
                kind, bank = use[0], n % 8
                if "d" in A_READ[kind]:
                    dve.wait_ge(a_pe, n + 1)
                    if "a" in A_READ[kind]:
                        dve.wait_ge(a_act, A_ACT[n + 1])
                if kind == "xt":
                    tok = slice(2 * P * use[1], 2 * P * (use[1] + 1))
                    dve.tensor_tensor(xt_lo[:, :, tok], ps[:, bank, :].rearrange("p (k t) -> p k t", k=KC),
                                      xt_hi[:, :, tok].bitcast(F32), ALU.subtract).then_inc(a_dve, 1)
                elif kind == "wt":
                    w = use[1]
                    hi, lo = (w_hi[:, w], w_lo[:, w]) if w < 3 else (wo_hi[:], wo_lo[:])
                    dve.tensor_tensor(lo, ps[:, bank, :].rearrange("p (k t) -> p k t", k=KC), hi.bitcast(F32),
                                      ALU.subtract).then_inc(a_dve, 1)
                elif kind == "bt":
                    dve.tensor_copy(bt[:, use[1]], ps[:, bank, 0:3 * P].rearrange("p (j f) -> p j f", j=3)).then_inc(a_dve, 1)
                elif kind == "proj":
                    _, w, hf, c = use
                    cols = slice(hf * BANK, hf * BANK + BANK)
                    if w == 1:
                        dve.wait_ge(a_pe, a_index[("dirp", 0, hf, c)] + 1)
                    dve.tensor_copy(lin[:, c, cols], ps[:, bank, :])
                    dve.scalar_tensor_tensor(out=base_lo[w][:, c, cols], in0=ps[:, bank, :],
                                             scalar=SCALE if w == 0 else 1.0, in1=base_hi[w][:, c, cols].bitcast(F32),
                                             op0=ALU.mult, op1=ALU.subtract).then_inc(a_dve, 1)
                elif kind == "dirp":
                    _, w, hf, c = use
                    cols = slice(hf * BANK, hf * BANK + BANK)
                    dve.wait_ge(a_act, A_ACT[n + 1])
                    link(dve.tensor_scalar(dirp[:, c, cols], dirp[:, c, cols], spk[:, c, 11 if w == 0 else 9:][:, 0:1],
                                           spk[:, c, 10:11], ALU.mult, ALU.add))
                    if w == 0:
                        dve.scalar_tensor_tensor(out=gauss[:, c, cols], in0=gauss[:, c, cols], scalar=spk[:, c, 12:13],
                                                 in1=dirp[:, c, cols], op0=ALU.mult, op1=ALU.mult).then_inc(feat_f, 1)
                    else:
                        dve.tensor_tensor(gauss[:, c, cols], gauss[:, c, cols], dirp[:, c, cols], ALU.mult).then_inc(feat_f, 1)

            for r, it in enumerate(ring):
                slot = 2 * (r % 2)
                if it[0] == "turn_max":
                    dve.wait_ge(ring_free, r)
                    link(dve.tensor_tensor(mpart[:, 0, TPG:T], mpart[:, 0, TPG:T], mpart[:, 1, TPG:T], ALU.max))
                    plain = mpart[:, 0, :, :, 0].rearrange("p t h -> p h t")
                    guided = mpart[:, 0, :, :, 1].rearrange("p t h -> p h t")
                    dve.tensor_scalar(mdiff[:, 0], plain, -1.0, None, ALU.mult)
                    link(dve.tensor_tensor(mdiff[:, 1], plain, guided, ALU.subtract))
                    if it[1] >= 1:
                        dve.wait_ge(ring_full, ring_at[("turn_max", it[1] - 1)] + 1)
                    link(dve.tensor_copy(mrow[:, :, 0].bitcast(F32R), mdiff[:]))
                    dve.tensor_tensor(mrow[:, :, 1].bitcast(F32R), mdiff[:], mrow[:, :, 0], ALU.subtract).then_inc(rows_ready, 1)
                dve.wait_ge(ring_full, r + 1)
                if it[0] == "max":
                    _, p, hh, i, c = it
                    n = min(BANK, (i + 1) * P - BANK * c)
                    dve.tensor_reduce(mpart[:, c, i, hh, :], ps[:, slot:slot + 2, 0:n], AX, ALU.max).then_inc(ring_free, 1)
                elif it[0] == "turn_max":
                    if it[1] >= 2:
                        dve.wait_ge(m_loaded, 32 * (it[1] - 1))
                    dve.tensor_copy(m_t[:, it[1] % 2, :], ps[0:64, slot, 0:P]).then_inc(ring_free, 1)
                else:
                    _, p, g = it
                    sums_v = ps[:, slot, :].rearrange("p (a e) -> p a e", e=32)
                    link(dve.reciprocal(rec[:].unsqueeze(2), sums_v[:, :, HD:HD + 1]))
                    link(dve.tensor_tensor(rw[:], rec[:], blend[:].rearrange("p a v -> p (a v)"), ALU.mult))
                    dve.tensor_tensor(otmp[:].rearrange("p t h v d -> p (t h v) d"), sums_v[:, :, 0:HD],
                                      rw[:].unsqueeze(2).broadcast_to([P, 16, HD]), ALU.mult).then_inc(ring_free, 1)
                    dve.wait_ge(ring_free, r + 1)
                    dst = attn[:, TPG * g:TPG * (g + 1), :].rearrange("p t (h e) -> p t h e", h=KC)
                    dve.tensor_tensor(dst[:, :, :, HD * p:HD * (p + 1)], otmp[:, :, :, 0, :], otmp[:, :, :, 1, :],
                                      ALU.add).then_inc(attn_done, 1)

            def variance(t, src):
                link(dve.bn_stats(stats[:, t, :], src[:, t, :]))
                link(dve.bn_aggr(mv[:, t, :], stats[:, t, :]))

            def add_eps(hf):
                dve.tensor_scalar(rstd[:, 4 * hf:4 * hf + 4, 0:1], mv[:, 4 * hf:4 * hf + 4, 1:2], EPS, None,
                                  ALU.add).then_inc(var_ready, 1)

            def normalize(hf, src, dst, count, done):
                dve.wait_ge(std_ready, count)
                link(dve.reciprocal(rstd[:, 4 * hf:4 * hf + 4, 2:3], rstd[:, 4 * hf:4 * hf + 4, 1:2]))
                for t in range(4 * hf, 4 * hf + 4):
                    dve.tensor_scalar(dst[:, t, :], src[:, t, :], mv[:, t, 0:1], rstd[:, t, 2:3],
                                      ALU.subtract, ALU.mult).then_inc(done, 1)

            for n, use in enumerate(F_USES):
                kind, bank = use[0], n % 8
                if kind == "yt" and use[1] == 0:
                    normalize(0, y, y, 1, y_ready)
                    normalize(1, y, y, 2, y_ready)
                if "d" not in F_READ[kind]:
                    continue
                dve.wait_ge(f_pe, n + 1)
                if "a" in F_READ[kind]:
                    dve.wait_ge(f_act, F_ACT[n + 1])
                if kind in ("at", "yt"):
                    tok = slice(2 * P * use[1], 2 * P * (use[1] + 1))
                    hi, lo = (at_hi, at_lo) if kind == "at" else (yt_hi, yt_lo)
                    dve.tensor_tensor(lo[:, :, tok], ps[:, bank, :].rearrange("p (k t) -> p k t", k=KC),
                                      hi[:, :, tok].bitcast(F32), ALU.subtract).then_inc(f_dve, 1)
                elif kind == "wo":
                    t = 2 * use[1]
                    dve.tensor_tensor(y[:, t:t + 2, :], ps[:, bank, :].rearrange("p (t d) -> p t d", t=2),
                                      x_sb[:, t:t + 2, :], ALU.add).then_inc(f_dve, 1)
                    dve.wait_ge(f_dve, F_DVE[n + 1])
                    variance(t, y)
                    variance(t + 1, y)
                    if use[1] % 2 == 1:
                        add_eps(use[1] // 2)
                elif kind == "up":
                    _, nn, s, c = use
                    u = nn * SETS + s
                    dve.wait_ge(f_act, F_ACT[n])
                    if u >= 2 and c == 0:
                        dve.wait_ge(sparse_lo, 4 * (u - 1))
                    dve.tensor_tensor(hid[:, u % 2, c, :], ps[:, bank, :], sg[:, (4 * u + c) % 2, :],
                                      ALU.mult).then_inc(f_dve, 1)
                    if c == 3:
                        sparsify(dve, link, u)
                else:
                    t = 2 * use[1]
                    dve.tensor_tensor(x_sb[:, t:t + 2, :], ps[:, bank, :].rearrange("p (t d) -> p t d", t=2),
                                      y[:, t:t + 2, :], ALU.add).then_inc(f_dve, 1)
                    dve.wait_ge(f_dve, F_DVE[n + 1])
                    variance(t, x_sb)
                    variance(t + 1, x_sb)
                    if use[1] % 2 == 1:
                        add_eps(use[1] // 2)
            normalize(0, x_sb, x_sb, 3, out_ready)
            normalize(1, x_sb, x_sb, 4, out_ready)


_INS = ["L0_attn_hidden_states", "L0_attn_Wq", "L0_attn_Wk", "L0_attn_Wv", "L0_attn_Wo",
        "L0_attn_splat_positions", "L0_attn_splat_directions", "L0_attn_splat_log_scales",
        "L0_attn_splat_log_amplitudes", "L0_attn_directional_strength", "L0_attn_position_sensitivity",
        "L0_attn_gsa_strength", "L0_ffn_w_gate", "L0_ffn_w_up", "L0_ffn_w_down"]


def kernel(**inputs):
    import numpy as _np
    import concourse.bacc as _bacc
    from concourse import mybir as _mybir
    from concourse.bass_utils import run_bass_kernel_spmd as _run

    nc = _bacc.Bacc("TRN2", target_bir_lowering=False, num_devices=1)
    arrays, args = {}, []
    for name in _INS:
        a = _np.ascontiguousarray(inputs[name])
        if a.ndim == 0:
            a = a.reshape(1)
        arrays[f"in_{name}_dram"] = a
        args.append(nc.dram_tensor(f"in_{name}_dram", a.shape, _mybir.dt.from_np(a.dtype), kind="ExternalInput").ap())
    out = nc.dram_tensor("out_0_dram", (1, 1024, 256), _mybir.dt.float32, kind="ExternalOutput").ap()
    build_kernel(nc, *args, out)
    r = _run(nc, [arrays], core_ids=[0])
    return r.results[0]["out_0_dram"]
```

```python
from contextlib import ExitStack

import concourse.bass as bass
from concourse import mybir

F32 = mybir.dt.float32
F32R = mybir.dt.float32r
BF16 = mybir.dt.bfloat16
ALU = mybir.AluOpType
ACT = mybir.ActivationFunctionType
AX = mybir.AxisListType.X

P = 128
BANK = 512
EPS = 1e-5
MASKED = -1e30


def build_kernel(nc, X, WQ, WK, WV, WO, POS, DIR, LSC, LAM, DST, PSE, GSA, WG, WU, WD, OUT):
    _, S, D = X.shape
    H, NS, HD = POS.shape
    I = WG.shape[1]
    T = S // P
    KC = D // P
    PAIRS = H // KC
    HPC = H // KC
    G = S // BANK
    TPG = BANK // P
    SPL = 2 * NS
    assert KC == 2 and SPL == HD and HPC * HD == P and G == 2
    ROWS = 3 * (HD + SPL)
    MROW = ROWS
    SROWS = ROWS + 4
    NB = 3
    NP = 3
    SETS = I // (4 * P)
    HC = I // P
    SCALE = float(HD) ** -0.5

    steps = [(p, g, kt) for p in range(PAIRS) for g in range(G) for kt in range(TPG * (g + 1))]
    SPP = len(steps) // PAIRS

    def q_offset(g, kt):
        return max(0, kt - TPG * g) * P

    HALF = BANK // 2

    def score_parts(g, kt):
        d = q_offset(g, kt)
        if kt < TPG * g:
            cut = [(0, BANK, 0, BANK, None)]
        elif d == 0:
            cut = [(0, HALF, 0, HALF, d), (HALF, HALF, HALF, BANK, None)]
        elif d < HALF:
            cut = [(d, HALF, d, d + HALF, d), (HALF, HALF, d + HALF, BANK, None)]
        else:
            cut = [(HALF, HALF, d, BANK, d)]
        return [(hh, v, *part) for hh in range(KC) for part in cut
                for v in ([(0, 1)] if part[1] <= HALF else [(0,), (1,)])]

    parts = [score_parts(g, kt) for _, g, kt in steps]
    parts_by = [sum(len(x) for x in parts[:s]) for s in range(len(steps) + 1)]

    def row_pieces(i):
        if i == 0:
            return [(0, HALF, P)]
        rest = (i - 1) * P
        wide = rest if rest <= BANK else (BANK if rest % HALF == 0 else rest - HALF)
        return ([((i - 1) * P, HALF, HALF)] + ([(0, max(wide, HALF), wide)] if rest else [])
                + ([(wide, HALF, HALF)] if rest > wide else []))

    PIECES = max(len(row_pieces(i)) for i in range(T))

    def row_items(p):
        return [("max", p, hh, i, c, v, nv) for hh in range(KC) for i in range(T)
                for c, piece in enumerate(row_pieces(i))
                for v, nv in (((0, 2),) if piece[1] <= HALF else ((0, 1), (1, 1)))]

    per_pair = len(row_items(0))
    cost_t = [BANK - min(q_offset(g, kt), BANK // 2) for _, g, kt in steps]
    stream = [it for p in range(PAIRS) for it in row_items(p)]
    cost_m = [nv * row_pieces(i)[c][1] for _, _, _, i, c, _, nv in stream]
    NR = 4
    NSC = 7 - NR
    LEAD = 10
    TURN_LAG = 4
    before = stream[:per_pair] + [("rows", 0)] + stream[per_pair:per_pair + TURN_LAG] + [("turn_max", 0)] + stream[per_pair + TURN_LAG:per_pair + LEAD]
    at_step = [[] for _ in steps]
    sent = per_pair + LEAD
    total_t, total_m = float(sum(cost_t)), float(sum(cost_m))
    m_start, run_t = float(sum(cost_m[:sent])), 0.0
    run_m = m_start
    turn_in = -1
    for s in range(len(steps)):
        run_t += cost_t[s]
        here = at_step[s]
        while sent < len(stream) and run_m - m_start < run_t * total_m / total_t:
            here.append(stream[sent])
            run_m += cost_m[sent]
            sent += 1
            if sent % per_pair == 0:
                here.append(("rows", sent // per_pair - 1))
                turn_in = TURN_LAG
            elif turn_in > 0:
                turn_in -= 1
                if turn_in == 0:
                    here.append(("turn_max", sent // per_pair - 1))
        if sent == len(stream) and turn_in > 0:
            turn_in = 0
            at_step[s + 1].append(("turn_max", PAIRS - 1))
        p, g, kt = steps[s]
        if g == 1 and kt == 1:
            here.append(("turn_out", p, 0))
        if p == PAIRS - 1 and g == 1:
            here += {2: [("at", 0), ("at", 1)], 3: [("wo", 0), ("wo", 1)], 7: [("yt", 0), ("yt", 1)]}.get(kt, [])
        if g == 0 and kt == 3 and p > 0:
            here.append(("turn_out", p - 1, 1))
    assert sent == len(stream) and turn_in <= 0
    after = [("turn_out", PAIRS - 1, 1)]
    vector_items = before + [it for here in at_step for it in here] + after
    ring = [it for it in vector_items if it[0] != "rows"]
    ring_at = {it: r for r, it in enumerate(ring)}

    with ExitStack() as ctx:
        def sem(name):
            return ctx.enter_context(nc.semaphore(name))

        def sb(name, shape, dt, own=ctx, **kw):
            return own.enter_context(nc.sbuf_tensor(name, shape, dt, **kw))

        ps = ctx.enter_context(nc.psum_tensor("ps", [P, 8, BANK], F32))

        x_sb = sb("x_sb", [P, T, D], F32)
        ident = sb("ident", [P, P], F32)
        ident_bf = sb("ident_bf", [P, P], BF16)
        causal = sb("causal", [P, P], BF16)
        wo_hi = sb("wo_hi", [P, KC, D], F32R)
        wo_lo = sb("wo_lo", [P, KC, D], F32R)
        vx = sb("vx", [P, T, H, 32], F32)
        attn = sb("attn", [P, T, D], F32)
        o_sb = sb("o_sb", [P, 2, BANK], F32)
        mpart = sb("mpart", [P, PIECES, T, KC, 2], F32)
        mdiff = sb("mdiff", [P, 2, KC, T], F32)
        mrow = sb("mrow", [P, 2, 2, KC, T], F32)
        m_t = sb("m_t", [64, 2, P], F32)
        rec = sb("rec", [P, 16], F32)
        rw = sb("rw", [P, 16], F32)
        otmp = sb("otmp", [P, TPG, KC, 2, HD], F32)
        sc = sb("sc", [P, 8], F32)
        blend = sb("blend", [P, 8, 2], F32)
        par = sb("par", [P, 2 * HD + 2], F32)
        spread_rows = sb("spread_rows", [P, KC, HPC, 2, NS], F32)
        spar = sb("spar", [P, KC, 2 * HD + 2], F32)
        spl = spar[:, :, 0:2 * HD].rearrange("p c (j d) -> p c j d", j=2)
        spk = sb("spk", [P, KC, 16], F32)
        spt = sb("spt", [P, KC, 3, HD], F32)
        spsq = sb("spsq", [P, KC, 2, HD], F32)
        half = sb("half", [P, HPC], F32)
        stats = sb("stats", [P, T, 6], F32)
        mv = sb("mv", [P, T, 2], F32)
        rstd = sb("rstd", [P, T, 3], F32)
        first = ExitStack()
        k_st = [sb("k_st0", [P, KC, S], F32R, first)]
        q_st = [sb("q_st0", [P, KC, S], F32R, first)]
        s_st = [sb("s_st0", [P, KC, S], F32R, first)]

        right = ExitStack()
        base_hi = [sb(f"base_hi{n}", [P, KC, S], F32R, right, side="right") for n in "qk"]
        base_lo = [sb(f"base_lo{n}", [P, KC, S], F32R, right, side="right") for n in "qk"]
        feat_hi = [sb(f"feat_hi{n}", [P, KC, S], F32R, right, side="right") for n in "qk"]
        feat_lo = [sb(f"feat_lo{n}", [P, KC, S], F32R, right, side="right") for n in "qk"]
        right.close()
        wg_hi = sb("wg_hi", [P, KC, SETS, 4, P], F32R, side="right")
        wg_lo = sb("wg_lo", [P, KC, SETS, 4, P], F32R, side="right")
        wu_hi = sb("wu_hi", [P, KC, SETS, 4, P], F32R, side="right")
        wu_lo = sb("wu_lo", [P, KC, SETS, 4, P], F32R, side="right")
        wd_hi = sb("wd_hi", [P, HC, D], F32R, side="right")
        wd_lo = sb("wd_lo", [P, HC, D], F32R, side="right")
        unsplit = ExitStack()
        raw = [sb(f"raw{n}", [P, 2 * I], F32, unsplit, side="right") for n in range(2)]
        unsplit.close()
        ht_hi, ht_lo = [None] * 3, [None] * 3
        ht_hi[2] = sb("ht_hi2", [P, 4, BANK], F32R, side="right")
        ht_lo[2] = sb("ht_lo2", [P, 4, BANK], F32R, side="right")

        early = ExitStack()
        w_nat = sb("w_nat", [P, 4, KC, D], F32, early)
        w_hi = sb("w_hi", [P, 3, KC, D], F32R, early)
        w_lo = sb("w_lo", [P, 3, KC, D], F32R, early)
        xt_hi = sb("xt_hi", [P, KC, S], F32R, early)
        xt_lo = sb("xt_lo", [P, KC, S], F32R, early)
        lin = sb("lin", [P, KC, S], F32, early)
        sq = sb("sq", [P, KC, S], F32, early)
        gauss = sb("gauss", [P, KC, S], F32, early)
        dirp = sb("dirp", [P, KC, S], F32, early)
        xs = attn[:].rearrange("p t d -> p (t d)")[:, 0:KC * 3 * P].rearrange(
            "p (c j h d) -> p c j h d", c=KC, j=3, h=HPC)
        bt = sb("bt", [P, KC, 3, P], F32, early)
        early.close()
        mid = ExitStack()
        for n in range(1, NB):
            k_st.append(sb(f"k_st{n}", [P, KC, S], F32R, mid))
            q_st.append(sb(f"q_st{n}", [P, KC, S], F32R, mid))
            s_st.append(sb(f"s_st{n}", [P, KC, S], F32R, mid))
        pr = sb("pr", [P, NP, 4, BANK], F32, mid)
        mid.close()
        first.close()
        y = attn
        yt_hi = sb("yt_hi", [P, KC, S], F32R)
        yt_lo = sb("yt_lo", [P, KC, S], F32R)
        at_hi = sb("at_hi", [P, KC, BANK], F32R)
        at_lo = sb("at_lo", [P, KC, BANK], F32R)
        for n in range(2):
            ht_hi[n] = sb(f"ht_hi{n}", [P, 4, BANK], F32R)
            ht_lo[n] = sb(f"ht_lo{n}", [P, 4, BANK], F32R)
        sg = sb("sg", [P, 2, BANK], F32)
        hid = sb("hid", [P, 2, 4, BANK], F32)
        mag = vx[:, 0:4].rearrange("p t h e -> p t (h e)")
        beats = sb("beats", [P, 6, BANK], BF16)
        sums = sb("sums", [P, 4, BANK], BF16)
        wins = sb("wins", [P, 4, BANK], BF16)

        x_loaded, w_loaded, spl_loaded = sem("x_loaded"), sem("w_loaded"), sem("spl_loaded")
        consts = sem("consts")
        ident_cast = sem("ident_cast")
        spl_act, spl_dve = sem("spl_act"), sem("spl_dve")
        spread, by_row = sem("spread"), sem("by_row")
        a_pe, a_act, a_dve = sem("a_pe"), sem("a_act"), sem("a_dve")
        lin_read = sem("lin_read")
        feat_f, feat_h, feat_l = sem("feat_f"), sem("feat_h"), sem("feat_l")
        attn_done = sem("attn_done")
        reused = sem("reused")
        st_loaded = [sem(f"st_loaded{b}") for b in range(NB)]
        m_loaded = sem("m_loaded")
        ring_full, ring_free = sem("ring_full"), sem("ring_free")
        rows_ready = sem("rows_ready")
        s_full, exp_done = sem("s_full"), sem("exp_done")
        pv_done, o_evac = sem("pv_done"), sem("o_evac")
        chain = sem("chain")
        raw_loaded = [sem(f"raw_loaded{n}") for n in range(3)]
        prep = sem("prep")
        half_hi = sem("half_hi")
        f_pe, f_act, f_dve = sem("f_pe"), sem("f_act"), sem("f_dve")
        var_ready, std_ready, y_ready = sem("var_ready"), sem("std_ready"), sem("y_ready")
        mag_ready = sem("mag_ready")
        sparse_ready, sparse_hi, sparse_lo = sem("sparse_ready"), sem("sparse_hi"), sem("sparse_lo")
        out_ready, stored = sem("out_ready"), sem("stored")

        A_USES = ([("xt", b) for b in range(4)] + [("wt", 0), ("wt", 1), ("bt", 0), ("bt", 1)]
                  + [("proj", 0, hf, c) for hf in range(2) for c in range(2)] + [("wt", 2)]
                  + [(k, 0, hf, c) for hf in range(2) for c in range(2) for k in ("gauss", "dirp")]
                  + [("proj", 1, hf, c) for hf in range(2) for c in range(2)]
                  + [("v", 0), ("v", 1)]
                  + [(k, 1, hf, c) for hf in range(2) for c in range(2) for k in ("gauss", "dirp")]
                  + [("v", 2), ("v", 3), ("wt", 3)])
        A_READ = {"xt": "ad", "wt": "ad", "bt": "d", "proj": "ad", "gauss": "a", "dirp": "a", "v": "a"}
        def units(first, end):
            return [(k, m // (4 * SETS), m // 4 % SETS, m % 4) for m in range(first, end) for k in ("gate", "up")]

        F_ORDER = (units(0, 1) + [("turned",)] + units(1, 2) + [("at", 2), ("at", 3), ("wo", 2), ("wo", 3)]
                   + units(2, 3) + [("normed",)] + units(3, 4) + [("yt", 2), ("yt", 3)] + units(4, 8 * SETS)
                   + [("down", t) for t in range(T)])
        F_USES = [u for u in F_ORDER if u[0] not in ("turned", "normed")]
        LAST_TILES = [slice(0, 4), slice(4, 6), slice(6, 8)]
        F_READ = {"at": "ad", "wo": "d", "yt": "ad", "gate": "a", "up": "d", "down": "d"}

        def counted(uses, read, who):
            out = [0]
            for u in uses:
                out.append(out[-1] + (who in read[u[0]]))
            return out

        A_ACT, A_DVE = counted(A_USES, A_READ, "a"), counted(A_USES, A_READ, "d")
        F_ACT, F_DVE = counted(F_USES, F_READ, "a"), counted(F_USES, F_READ, "d")
        a_index = {u: n for n, u in enumerate(A_USES)}
        f_index = {u: n for n, u in enumerate(F_USES)}

        def hidden_count(m):
            return F_DVE[f_index[("up", m // (4 * SETS), m // 4 % SETS, m % 4)] + 1]

        def bank_free(pe, uses, read, acts, dves, act_sem, dve_sem, n):
            if n >= 8:
                if "a" in read[uses[n - 8][0]]:
                    pe.wait_ge(act_sem, acts[n - 7])
                if "d" in read[uses[n - 8][0]]:
                    pe.wait_ge(dve_sem, dves[n - 7])

        block = ctx.enter_context(nc.Block())

        @block.sync
        def _(sp):
            xv = X[0].rearrange("(t p) d -> p t d", p=P)
            sp.dma_start(x_sb[:, 0:4, :], xv[:, 0:4, :]).then_inc(x_loaded, 16)
            sp.dma_start(x_sb[:, 4:8, :], xv[:, 4:8, :]).then_inc(x_loaded, 16)

            def stack(p):
                b, r = p % NB, HD * p
                parts = ((q_st[b], base_hi[0], 0), (q_st[b], base_hi[0], 1), (q_st[b], base_lo[0], 2),
                         (q_st[b], feat_hi[0], 3), (q_st[b], feat_hi[0], 4), (q_st[b], feat_lo[0], 5),
                         (k_st[b], base_hi[1], 0), (k_st[b], base_lo[1], 1), (k_st[b], base_hi[1], 2),
                         (k_st[b], feat_hi[1], 3), (k_st[b], feat_lo[1], 4), (k_st[b], feat_hi[1], 5),
                         (s_st[b], base_hi[0], 0), (s_st[b], base_hi[0], 1), (s_st[b], base_lo[0], 2))
                for dst, src, n in parts:
                    sp.dma_start(dst[HD * n:HD * n + HD, :, :].bitcast(F32),
                                 src[r:r + HD, :, :].bitcast(F32)).then_inc(st_loaded[b], 16)

            def maxima(p):
                sp.wait_ge(ring_free, ring_at[("turn_max", p)] + 1)
                b = p % NB
                sp.dma_start(q_st[b][MROW:MROW + 4, :, :].bitcast(F32), m_t[0:64, p % 2, :]).then_inc(m_loaded, 16)
                sp.dma_start(s_st[b][MROW:MROW + 2, :, :].bitcast(F32), m_t[0:32, p % 2, :]).then_inc(m_loaded, 16)

            sp.wait_ge(consts, 6)
            sp.wait_ge(a_act, A_ACT[a_index[("proj", 1, 1, 1)] + 1])
            sp.wait_ge(a_dve, A_DVE[a_index[("proj", 1, 1, 1)] + 1])
            sp.wait_ge(feat_h, 8)
            sp.wait_ge(feat_l, 8)
            stack(0)
            sp.wait_ge(reused, 2 * (NB - 1))
            stack(1)
            stack(2)
            maxima(0)
            for p in range(PAIRS):
                if p + 1 < PAIRS:
                    maxima(p + 1)
                if p + 3 < PAIRS:
                    sp.wait_ge(s_full, parts_by[SPP * (p + 1)])
                    stack(p + 3)
                if p + 3 == PAIRS - 1:
                    for b in range(NB):
                        sp.wait_ge(st_loaded[b], 16 * 15 * len(range(b, PAIRS, NB)))
                    sp.dma_start(raw[0][:], WG.rearrange("(k p) i -> p k i", p=P)).then_inc(raw_loaded[0], 16)
                    sp.dma_start(raw[1][:], WU.rearrange("(k p) i -> p k i", p=P)).then_inc(raw_loaded[1], 16)
            sp.wait_ge(prep, 8)
            sp.dma_start(raw[0][:], WD.rearrange("(s j c) n -> j s c n", s=SETS, c=4)).then_inc(raw_loaded[2], 16)
            ov = OUT[0].rearrange("(t p) d -> p t d", p=P)
            for t in range(T):
                sp.wait_ge(out_ready, t + 1)
                sp.dma_start(ov[:, t, :], x_sb[:, t, :]).then_inc(stored, 16)
            sp.wait_ge(stored, 16 * T)

        @block.gpsimd
        def _(pool):
            pool.memset(ident[:], 0.0).then_inc(consts, 1)
            pool.memset(causal[:], 0.0).then_inc(consts, 1)
            pool.wait_ge(consts, 2)
            pool.affine_select(out=ident[:], in_=ident[:], compare_op=ALU.not_equal, fill=1.0, base=0,
                               pattern=[[-1, P]], channel_multiplier=1).then_inc(consts, 1)
            pool.affine_select(out=causal[:], in_=causal[:], compare_op=ALU.is_ge, fill=MASKED, base=0,
                               pattern=[[-1, P]], channel_multiplier=1).then_inc(consts, 1)
            pool.memset(spread_rows[:], 0.0).then_inc(spread, 1)
            pool.wait_ge(spread, 1)
            for c in range(KC):
                pool.affine_select(out=spread_rows[:, c], in_=spread_rows[:, c], compare_op=ALU.not_equal, fill=1.0,
                                   base=-HPC * NS * c, pattern=[[-NS, HPC], [0, 2], [-1, NS]],
                                   channel_multiplier=1).then_inc(spread, 1)
            pool.memset(s_st[0][:].bitcast(F32), 0.0).then_inc(consts, 1)
            pool.wait_ge(consts, 5)
            pool.memset(k_st[0][ROWS:SROWS].bitcast(F32), 1.0).then_inc(consts, 1)
            pool.wait_ge(consts, 6)
            pool.memset(half[:], 1.0).then_inc(consts, 1)
            pool.wait_ge(consts, 7)
            pool.affine_select(out=half[:], in_=half[:], compare_op=ALU.is_ge, fill=0.0, base=-NS,
                               pattern=[[-HD, HPC]], channel_multiplier=1).then_inc(consts, 1)
            pool.wait_ge(consts, 8)
            pool.affine_select(out=half[:], in_=half[:], compare_op=ALU.is_ge, fill=0.0, base=HD - 1,
                               pattern=[[HD, HPC]], channel_multiplier=-1).then_inc(consts, 1)
            pool.memset(vx[:, :, :, HD:32], 1.0).then_inc(consts, 1)
            pool.wait_ge(spread, 4)
            blocks = xs.rearrange("p c j h d -> p (c j) h d")
            pool.affine_select(out=blocks, in_=blocks, compare_op=ALU.is_ge, fill=0.0, base=0,
                               pattern=[[0, 6], [-HD, HPC], [0, HD]], channel_multiplier=1).then_inc(spread, 1)
            pool.wait_ge(spread, 5)
            pool.affine_select(out=blocks, in_=blocks, compare_op=ALU.is_ge, fill=0.0, base=HD - 1,
                               pattern=[[0, 6], [HD, HPC], [0, HD]], channel_multiplier=-1).then_inc(spread, 1)
            for n in range(8):
                w, hf, c = n // 4, n // 2 % 2, n % 2
                cols = slice(hf * BANK, hf * BANK + BANK)
                pool.wait_ge(feat_h, n + 1)
                pool.tensor_tensor(feat_lo[w][:, c, cols], gauss[:, c, cols], feat_hi[w][:, c, cols].bitcast(F32),
                                   ALU.subtract).then_inc(feat_l, 1)
            pool.wait_ge(a_pe, len(A_USES))
            pool.wait_ge(a_act, A_ACT[-1])
            pool.wait_ge(a_dve, A_DVE[-1])
            pool.wait_ge(feat_l, 8)
            for b in range(1, NB):
                pool.memset(s_st[b][:].bitcast(F32), 0.0).then_inc(reused, 1)
                pool.wait_ge(reused, 2 * b - 1)
                pool.memset(k_st[b][ROWS:SROWS].bitcast(F32), 1.0).then_inc(reused, 1)
                pool.wait_ge(reused, 2 * b)

            def slices():
                for n, (src, hi, lo) in enumerate(((raw[0], wg_hi, wg_lo), (raw[1], wu_hi, wu_lo))):
                    rv = src[:].rearrange("p (k s j c) -> p k s c j", k=KC, s=SETS, c=4)
                    for k in range(KC):
                        for s in range(SETS):
                            yield n, rv[:, k, s], hi[:, k, s], lo[:, k, s]
                rv = raw[0][:].rearrange("p (m n) -> p m n", m=HC)
                for m in range(0, HC, 2):
                    yield 2, rv[:, m:m + 2], wd_hi[:, m:m + 2], wd_lo[:, m:m + 2]

            for m, (n, src, hi, lo) in enumerate(slices()):
                pool.wait_ge(raw_loaded[n], 16)
                pool.tensor_scalar(hi, src, 1.0, 0.0, ALU.mult, ALU.add).then_inc(prep, 1)
                pool.wait_ge(prep, 2 * m + 1)
                pool.tensor_tensor(lo, src, hi.bitcast(F32), ALU.subtract).then_inc(prep, 1)
            for n in range(2):
                for s in range(SETS):
                    u = n * SETS + s
                    for c in range(4):
                        pool.wait_ge(sparse_hi, 4 * u + c + 1)
                        pool.tensor_tensor(ht_lo[u % 3][:, c, :], hid[:, u % 2, c, :],
                                           ht_hi[u % 3][:, c, :].bitcast(F32), ALU.subtract).then_inc(sparse_lo, 1)

        def magnitude(act, m):
            u, c = m // 4, m % 4
            act.wait_ge(f_dve, hidden_count(m))
            if c == 0 and u >= 1:
                act.wait_ge(sparse_ready, 4 * u)
            act.activation(mag[:, c, :], hid[:, u % 2, c, :], ACT.Abs).then_inc(mag_ready, 1)

        def highs(act, u):
            if u == 3:
                act.wait_ge(f_pe, f_index[("down", TPG - 1)] + 1)
            for c in range(4):
                act.wait_ge(sparse_ready, 4 * u + c + 1)
                act.activation(ht_hi[u % 3][:, c, :], hid[:, u % 2, c, :], ACT.Copy).then_inc(sparse_hi, 1)

        def deviation(act, n, tiles):
            act.wait_ge(var_ready, n)
            act.activation(rstd[:, tiles, 1:2], rstd[:, tiles, 0:1], ACT.Sqrt).then_inc(std_ready, 1)

        def high_half(act, kind, b, bank):
            dst, t = (at_hi, 2 * P * (b % 2)) if kind == "at" else (yt_hi, 2 * P * b)
            return act.activation(dst[:, :, t:t + 2 * P], ps[:, bank, :].rearrange("p (k t) -> p k t", k=KC), ACT.Copy)

        @block.scalar
        def _(act):
            for n, w in enumerate((WQ, WK, WV, WO)):
                act.dma_start(w_nat[:, n], w.rearrange("(c p) d -> p c d", p=P)).then_inc(w_loaded, 16)
            for v, cols in ((POS, slice(0, HD)), (DIR, slice(HD, 2 * HD))):
                act.dma_start(par[:, cols], v.rearrange("h n d -> (h n) d")).then_inc(spl_loaded, 16)
            for v, col in ((LSC, 2 * HD), (LAM, 2 * HD + 1)):
                act.dma_start(par[:, col:col + 1], v.rearrange("h (n o) -> (h n) o", o=1)).then_inc(spl_loaded, 16)
            for j, v in enumerate((DST, PSE, GSA)):
                act.dma_start(sc[:, j:j + 1], bass.AP(tensor=v.tensor, offset=0, ap=[[0, P], [1, 1]])).then_inc(spl_loaded, 16)
            act.wait_ge(spl_loaded, 16 * 7)
            act.wait_ge(spl_dve, 1)
            act.activation(spk[:, :, 2:3], spar[:, :, 2 * HD:2 * HD + 1], ACT.Exp, scale=-2.0)
            act.activation(spk[:, :, 3:4], spar[:, :, 2 * HD + 1:2 * HD + 2], ACT.Exp)
            act.activation(sc[:, 3:4], sc[:, 2:3], ACT.Exp, scale=-1.0).then_inc(spl_act, 1)
            act.wait_ge(spl_dve, 2)
            act.activation(spk[:, :, 5:6], spk[:, :, 4:5], ACT.Sqrt).then_inc(spl_act, 1)

            n_feat = 0
            for n, use in enumerate(A_USES):
                kind, bank = use[0], n % 8
                if "a" not in A_READ[kind]:
                    continue
                act.wait_ge(a_pe, n + 1)
                if kind == "xt":
                    b = use[1]
                    act.activation(xt_hi[:, :, 2 * P * b:2 * P * (b + 1)],
                                   ps[:, bank, :].rearrange("p (k t) -> p k t", k=KC), ACT.Copy).then_inc(a_act, 1)
                elif kind == "wt":
                    w = use[1]
                    dst = w_hi[:, w] if w < 3 else wo_hi[:]
                    act.activation(dst, ps[:, bank, :].rearrange("p (k t) -> p k t", k=KC), ACT.Copy).then_inc(a_act, 1)
                elif kind == "proj":
                    _, w, hf, c = use
                    cols = slice(hf * BANK, hf * BANK + BANK)
                    act.activation(base_hi[w][:, c, cols], ps[:, bank, :], ACT.Copy, scale=SCALE if w == 0 else 1.0)
                    if w == 1:
                        act.wait_ge(a_pe, a_index[("gauss", 0, hf, c)] + 1)
                    act.activation(sq[:, c, cols], ps[:, bank, :], ACT.Square).then_inc(a_act, 1)
                elif kind in ("gauss", "dirp"):
                    _, w, hf, c = use
                    cols = slice(hf * BANK, hf * BANK + BANK)
                    if kind == "gauss":
                        act.wait_ge(spl_dve, 3)
                        if w == 1:
                            act.wait_ge(feat_l, n_feat - 4 + 1)
                        act.activation(gauss[:, c, cols], ps[:, bank, :], ACT.Exp,
                                       bias=spk[:, c, 6:7]).then_inc(a_act, 1)
                    else:
                        if w == 1:
                            act.wait_ge(feat_f, n_feat - 4 + 1)
                        act.activation(dirp[:, c, cols], ps[:, bank, :], ACT.Tanh,
                                       bias=spk[:, c, 7:8]).then_inc(a_act, 1)
                        n_feat += 1
                        if n_feat % 4 != 1:
                            m = n_feat - 2
                            act.wait_ge(feat_f, m + 1)
                            mc = slice(m // 2 % 2 * BANK, (m // 2 % 2 + 1) * BANK)
                            act.activation(feat_hi[m // 4][:, m % 2, mc], gauss[:, m % 2, mc], ACT.Copy).then_inc(feat_h, 1)
                        if n_feat in (4, 8):
                            m = n_feat - 1
                            act.wait_ge(feat_f, m + 1)
                            mc = slice(m // 2 % 2 * BANK, (m // 2 % 2 + 1) * BANK)
                            act.activation(feat_hi[m // 4][:, m % 2, mc], gauss[:, m % 2, mc], ACT.Copy).then_inc(feat_h, 1)
                elif kind == "v":
                    t = 2 * use[1]
                    act.wait_ge(consts, 10)
                    act.activation(vx[:, t:t + 2, :, 0:HD],
                                   ps[:, bank, :].rearrange("p (t h d) -> p t h d", t=2, h=H), ACT.Copy).then_inc(a_act, 1)

            def evacuate(n):
                last = SPP * (n // G) + (TPG if n % G == 0 else SPP)
                act.wait_ge(pv_done, last)
                if n >= 2:
                    act.wait_ge(ring_full, ring_at[("turn_out", (n - 2) // G, n % G)] + 1)
                act.activation(o_sb[:, n % 2, :], ps[:, 7, :], ACT.Copy).then_inc(o_evac, 1)

            act.wait_ge(reused, 2 * (NB - 1))
            for s, (p, g, kt) in enumerate(steps):
                for t, (hh, vs, start, width, first_q, end_q, _) in enumerate(parts[s]):
                    n = parts_by[s] + t
                    act.wait_ge(s_full, n + 1)
                    if s >= NP and t == 0:
                        act.wait_ge(pv_done, s - NP + 1)
                    src = ps[:, NR + n % NSC, :].rearrange("p (v q) -> p v q", q=width)[:, :, first_q - start:end_q - start]
                    act.activation(pr[:, s % NP, 2 * hh + vs[0]:2 * hh + vs[-1] + 1, first_q:end_q], src,
                                   ACT.Exp).then_inc(exp_done, 1)
                if kt == 0 and s > 0:
                    evacuate(G * p + g - 1)
                if p == PAIRS - 1 and g == 1 and kt == 5:
                    deviation(act, 1, slice(0, TPG))
                for it in at_step[s]:
                    if it[0] in ("at", "yt"):
                        act.wait_ge(ring_full, ring_at[it] + 1)
                        high_half(act, it[0], it[1], ring_at[it] % NR).then_inc(half_hi, 1)
            evacuate(G * PAIRS - 1)

            made = marked = 0
            n = -1
            for use in F_ORDER:
                kind = use[0]
                if kind == "normed":
                    deviation(act, 2, slice(TPG, T))
                if kind in ("turned", "normed"):
                    continue
                n += 1
                bank = (n + NR) % 8
                if "a" not in F_READ[kind]:
                    continue
                if kind == "yt" and marked < made:
                    magnitude(act, marked)
                    marked += 1
                act.wait_ge(f_pe, n + 1)
                if kind in ("at", "yt"):
                    high_half(act, kind, use[1], bank).then_inc(f_act, 1)
                elif kind == "gate":
                    _, nn, s, c = use
                    u = nn * SETS + s
                    m = 4 * u + c
                    if m >= 2:
                        act.wait_ge(f_dve, hidden_count(m - 2))
                    act.activation(sg[:, m % 2, :], ps[:, bank, :], ACT.Silu).then_inc(f_act, 1)
                    if m > marked:
                        magnitude(act, marked)
                        marked += 1
                    made = m + 1
                    if c == 2 and u >= 1:
                        highs(act, u - 1)
            magnitude(act, 8 * SETS - 1)
            highs(act, 2 * SETS - 1)
            for m, tiles in enumerate(LAST_TILES):
                deviation(act, 3 + m, tiles)

        @block.tensor
        def _(pe):
            def three(out, lhs, rhs, first, last, **kw):
                pe.matmul(out, lhs[0], rhs[0], start=first, stop=False, **kw)
                pe.matmul(out, lhs[0], rhs[1], start=False, stop=False, **kw)
                return pe.matmul(out, lhs[1], rhs[0], start=False, stop=last, **kw)

            pe.wait_ge(consts, 4)
            for n, use in enumerate(A_USES):
                kind, bank = use[0], n % 8
                bank_free(pe, A_USES, A_READ, A_ACT, A_DVE, a_act, a_dve, n)
                if n == 4:
                    pe.wait_ge(spl_loaded, 16 * 7)
                    pe.wait_ge(spread, 3)
                    for c in range(KC):
                        mm = pe.matmul(ps[:, 7, c * (2 * HD + 2):(c + 1) * (2 * HD + 2)],
                                       spread_rows[:, c].rearrange("p h f n -> p (h f n)"), par[:], start=True, stop=True)
                    mm.then_inc(by_row, 1)
                if kind == "xt":
                    b = use[1]
                    pe.wait_ge(x_loaded, 32)
                    for k in range(KC):
                        for t in range(2):
                            o = (2 * k + t) * P
                            mm = pe.transpose(ps[:, bank, o:o + P], x_sb[:, 2 * b + t, P * k:P * (k + 1)], ident[:])
                elif kind == "wt":
                    w = use[1]
                    pe.wait_ge(w_loaded, 64)
                    for k in range(KC):
                        for c in range(KC):
                            o = (2 * k + c) * P
                            mm = pe.transpose(ps[:, bank, o:o + P], w_nat[:, w, c, P * k:P * (k + 1)], ident[:])
                elif kind == "bt":
                    c = use[1]
                    pe.wait_ge(spread, 6)
                    for j in range(3):
                        mm = pe.transpose(ps[:, bank, j * P:(j + 1) * P],
                                          xs[:, c, j].rearrange("p h d -> p (h d)"), ident[:])
                elif kind == "proj":
                    _, w, hf, c = use
                    cols = slice(hf * BANK, hf * BANK + BANK)
                    dims = slice(P * c, P * c + P)
                    pe.wait_ge(a_dve, A_DVE[a_index[("wt", w)] + 1])
                    for k in range(KC):
                        mm = three(ps[:, bank, :], (w_hi[:, w, k, dims], w_lo[:, w, k, dims]),
                                   (xt_hi[:, k, cols], xt_lo[:, k, cols]), k == 0, k == KC - 1)
                elif kind == "gauss":
                    _, w, hf, c = use
                    cols = slice(hf * BANK, hf * BANK + BANK)
                    pe.wait_ge(a_dve, A_DVE[a_index[("proj", w, hf, c)] + 1])
                    pe.wait_ge(a_dve, A_DVE[a_index[("bt", 1)] + 1])
                    pe.matmul(ps[:, bank, :], bt[:, c, 0], lin[:, c, cols], start=True, stop=False)
                    mm = pe.matmul(ps[:, bank, :], bt[:, c, 2], sq[:, c, cols], start=False, stop=True)
                elif kind == "dirp":
                    _, w, hf, c = use
                    mm = pe.matmul(ps[:, bank, :], bt[:, c, 1], lin[:, c, hf * BANK:hf * BANK + BANK],
                                   start=True, stop=True)
                elif kind == "v":
                    pe.wait_ge(a_dve, A_DVE[a_index[("wt", 2)] + 1])
                    for j in range(2):
                        t = 2 * use[1] + j
                        tok = slice(P * t, P * t + P)
                        for k in range(KC):
                            mm = three(ps[:, bank, j * D:(j + 1) * D], (xt_hi[:, k, tok], xt_lo[:, k, tok]),
                                       (w_hi[:, 2, k, :], w_lo[:, 2, k, :]), k == 0, k == KC - 1)
                mm.then_inc(a_pe, 1)
            pe.wait_ge(a_act, A_ACT[-1])
            pe.wait_ge(a_dve, A_DVE[-1])
            pe.wait_ge(ident_cast, 1)

            def turn_tiles(kind, b, bank):
                src = attn if kind == "at" else y
                for k in range(KC):
                    for t in range(2):
                        o = (2 * k + t) * P
                        mm = pe.transpose(ps[:, bank, o:o + P], src[:, 2 * b + t, P * k:P * (k + 1)], ident[:])
                return mm

            def project_out(b, bank):
                for j in range(2):
                    tok = slice(P * (2 * (b % 2) + j), P * (2 * (b % 2) + j + 1))
                    for k in range(KC):
                        mm = three(ps[:, bank, j * D:(j + 1) * D], (at_hi[:, k, tok], at_lo[:, k, tok]),
                                   (wo_hi[:, k, :], wo_lo[:, k, :]), k == 0, k == KC - 1)
                return mm

            def down(t, u, bank):
                tok = slice(P * (t % TPG), P * (t % TPG + 1))
                for c in range(4):
                    m = 4 * (u % SETS) + c
                    mm = three(ps[:, bank, 0:D], (ht_hi[u % 3][:, c, tok], ht_lo[u % 3][:, c, tok]),
                               (wd_hi[:, m, :], wd_lo[:, m, :]), m == 0, m == HC - 1)
                return mm

            def item(it):
                if it[0] == "rows":
                    return
                r = ring_at[it]
                slot = r % NR
                if r >= NR:
                    pe.wait_ge(ring_free, r - NR + 1)
                if it[0] == "max":
                    _, p, hh, i, c, v0, nv = it
                    b = p % NB
                    if hh == 0 and i == 0 and v0 == 0:
                        pe.wait_ge(st_loaded[b], 16 * 15 * (p // NB + 1))
                    first, n, _ = row_pieces(i)[c]
                    for v in range(v0, v0 + nv):
                        at = (v - v0) * n
                        mm = pe.matmul(ps[:, slot, at:at + n], (s_st[b], q_st[b])[v][0:ROWS, hh, i * P:(i + 1) * P],
                                       k_st[b][0:ROWS, hh, first:first + n], start=(v == v0), stop=True,
                                       skip_group_check=(v > v0))
                    if c == 0:
                        both = ps[:, slot, :].rearrange("p (v n) -> p v n", v=2)
                        at = i * P - first
                        mm = pe.matmul(both[:, :, at:at + P], ident_bf[:], causal[:].unsqueeze(1).broadcast_to([P, 2, P]),
                                       start=False, stop=True, skip_group_check=True)
                elif it[0] == "turn_max":
                    p = it[1]
                    pe.wait_ge(rows_ready, p + 1)
                    mm = pe.transpose(ps[0:64, slot, 0:P], mrow[:].rearrange("p a b h t -> p (a b h t)"), ident[:])
                elif it[0] in ("at", "yt"):
                    if it[0] == "at":
                        pe.wait_ge(attn_done, G * PAIRS - 1)
                    else:
                        pe.wait_ge(y_ready, 2 * it[1] + 2)
                    mm = turn_tiles(it[0], it[1], slot)
                elif it[0] == "wo":
                    pe.wait_ge(ring_free, ring_at[("at", it[1])] + 1)
                    mm = project_out(it[1], slot)
                else:
                    _, p, g = it
                    n = G * p + g
                    pe.wait_ge(o_evac, n + 1)
                    for t in range(TPG):
                        mm = pe.transpose(ps[:, slot, t * P:(t + 1) * P], o_sb[:, n % 2, t * P:(t + 1) * P], ident[:])
                mm.then_inc(ring_full, 1)

            def values(s):
                p, g, kt = steps[s]
                off = q_offset(g, kt)
                pe.wait_ge(exp_done, parts_by[s + 1])
                if kt == 0 and s > 0:
                    pe.wait_ge(o_evac, G * p + g)
                for t in range(4):
                    mm = pe.matmul(ps[32 * t:32 * t + 32, 7, off:BANK], vx[:, kt, p + HPC * (t // 2), :],
                                   pr[:, s % NP, t, off:BANK], start=(kt == 0), stop=(kt == TPG * (g + 1) - 1),
                                   skip_group_check=True)
                mm.then_inc(pv_done, 1)

            for it in before:
                item(it)
            def scores(s, t):
                p, g, kt = steps[s]
                b, n = p % NB, parts_by[s] + t
                hh, vs, start, width, _, _, diagonal = parts[s][t]
                bank = NR + n % NSC
                if s % SPP == 0 and t == 0:
                    pe.wait_ge(m_loaded, 32 * (p + 1))
                if n >= NSC:
                    pe.wait_ge(exp_done, n - NSC + 1)
                for j, v in enumerate(vs):
                    q = g * BANK + start
                    mm = pe.matmul(ps[:, bank, j * width:(j + 1) * width], k_st[b][0:SROWS, hh, kt * P:(kt + 1) * P],
                                   (s_st[b], q_st[b])[v][0:SROWS, hh, q:q + width], start=(j == 0), stop=True,
                                   skip_group_check=(j > 0))
                if diagonal is not None:
                    both = ps[:, bank, :].rearrange("p (v q) -> p v q", v=2)
                    at = diagonal - start
                    mm = pe.matmul(both[:, :, at:at + P], causal[:], ident_bf[:].unsqueeze(1).broadcast_to([P, 2, P]),
                                   start=False, stop=True, skip_group_check=True)
                mm.then_inc(s_full, 1)

            for s in range(len(steps)):
                mine = list(at_step[s])
                for t in range(len(parts[s])):
                    scores(s, t)
                    for _ in range(4 // len(parts[s])):
                        if mine:
                            item(mine.pop(0))
                for it in mine:
                    item(it)
                if s >= 1:
                    values(s - 1)
            values(len(steps) - 1)
            pe.wait_ge(exp_done, parts_by[-1])
            pe.wait_ge(ring_free, ring_at[("yt", 1)] + 1)
            pe.wait_ge(prep, 24)
            n = -1
            for use in F_ORDER:
                kind = use[0]
                if kind == "turned":
                    item(after[-1])
                if kind in ("turned", "normed"):
                    continue
                n += 1
                bank = (n + NR) % 8
                if bank == 7 and n < 8:
                    pe.wait_ge(o_evac, G * PAIRS)
                elif bank < NR and n < 8:
                    pe.wait_ge(ring_free, max(r for r in range(len(ring)) if r % NR == bank) + 1)
                bank_free(pe, F_USES, F_READ, F_ACT, F_DVE, f_act, f_dve, n)
                if kind in ("at", "yt"):
                    if kind == "at":
                        pe.wait_ge(attn_done, G * PAIRS)
                    else:
                        pe.wait_ge(y_ready, 2 * use[1] + 2)
                    mm = turn_tiles(kind, use[1], bank)
                elif kind == "wo":
                    pe.wait_ge(f_dve, F_DVE[f_index[("at", use[1])] + 1])
                    mm = project_out(use[1], bank)
                elif kind in ("gate", "up"):
                    _, nn, s, c = use
                    cols = slice(nn * BANK, nn * BANK + BANK)
                    if nn == 1:
                        pe.wait_ge(f_dve, F_DVE[f_index[("yt", 3)] + 1])
                    hi, lo = (wg_hi, wg_lo) if kind == "gate" else (wu_hi, wu_lo)
                    for k in range(KC):
                        mm = three(ps[:, bank, :], (hi[:, k, s, c], lo[:, k, s, c]),
                                   (yt_hi[:, k, cols], yt_lo[:, k, cols]), k == 0, k == KC - 1)
                else:
                    t = use[1]
                    if t < TPG:
                        pe.wait_ge(sparse_lo, 4 * SETS)
                        for u in range(SETS):
                            mm = down(t, u, bank)
                    else:
                        if t == TPG:
                            pe.wait_ge(sparse_lo, 4 * 3)
                            for j in range(TPG):
                                if j > 0:
                                    bank_free(pe, F_USES, F_READ, F_ACT, F_DVE, f_act, f_dve, n + j)
                                down(t + j, 2, (n + j + NR) % 8)
                            pe.wait_ge(sparse_lo, 4 * 4)
                        mm = down(t, 3, bank)
                mm.then_inc(f_pe, 1)

        def sparsify(dve, link, u):
            h = hid[:, u % 2]
            dve.wait_ge(mag_ready, 4 * u + 4)
            dve.tensor_tensor(beats[:, 0:3, :], mag[:, 0:1, :].broadcast_to([P, 3, BANK]), mag[:, 1:4, :], ALU.is_ge)
            dve.tensor_tensor(beats[:, 3:5, :], mag[:, 1:2, :].broadcast_to([P, 2, BANK]), mag[:, 2:4, :], ALU.is_ge)
            link(dve.tensor_tensor(beats[:, 5, :], mag[:, 2, :], mag[:, 3, :], ALU.is_ge))
            dve.tensor_tensor(sums[:, 0:2, :], beats[:, 0:4:3, :], beats[:, 1:5:3, :], ALU.add)
            link(dve.tensor_tensor(sums[:, 2:4, :], beats[:, 1:3, :], beats[:, 3:5, :], ALU.add))
            dve.tensor_tensor(wins[:, 0:4:3, :], sums[:, 0:4:3, :], beats[:, 2:6:3, :], ALU.add)
            link(dve.tensor_tensor(wins[:, 1:3, :], sums[:, 1:3, :], beats[:, 0:6:5, :], ALU.subtract))
            for c, (limit, op) in enumerate(((2.0, ALU.is_ge), (1.0, ALU.is_ge), (0.0, ALU.is_le), (1.0, ALU.is_le))):
                dve.scalar_tensor_tensor(out=h[:, c, :], in0=wins[:, c, :], scalar=limit, in1=h[:, c, :],
                                         op0=op, op1=ALU.mult).then_inc(sparse_ready, 1)

        @block.vector
        def _(dve):
            links = [0]

            def link(ins):
                links[0] += 1
                ins.then_inc(chain, 1)
                dve.wait_ge(chain, links[0])

            dve.wait_ge(consts, 4)
            dve.tensor_copy(ident_bf[:], ident[:]).then_inc(ident_cast, 1)
            dve.wait_ge(spl_loaded, 16 * 7)
            dve.wait_ge(by_row, 1)
            dve.tensor_copy(spar[:], ps[:, 7, 0:KC * (2 * HD + 2)].rearrange("p (c e) -> p c e", c=KC)).then_inc(spl_dve, 1)
            dve.wait_ge(spl_dve, 1)
            dve.tensor_tensor(spsq[:, :, 1, :], spl[:, :, 1, :], spl[:, :, 1, :], ALU.mult)
            link(dve.tensor_tensor(spsq[:, :, 0, :], spl[:, :, 0, :], spl[:, :, 0, :], ALU.mult))
            dve.wait_ge(spl_act, 1)
            dve.tensor_reduce(spk[:, :, 8:9], spsq[:, :, 0, :], AX, ALU.add)
            dve.tensor_reduce(spk[:, :, 4:5], spsq[:, :, 1, :], AX, ALU.add).then_inc(spl_dve, 1)
            link(dve.tensor_scalar(sc[:, 4:5], sc[:, 3:4], 1.0, None, ALU.add))
            link(dve.reciprocal(sc[:, 5:6], sc[:, 4:5]))
            link(dve.tensor_scalar(sc[:, 6:7], sc[:, 5:6], 0.15, 0.03, ALU.mult, ALU.min))
            dve.tensor_copy(blend[:, :, 1:2], sc[:, 6:7].unsqueeze(1).broadcast_to([P, 8, 1]))
            dve.tensor_scalar(blend[:, :, 0:1], sc[:, 6:7].unsqueeze(1).broadcast_to([P, 8, 1]), -1.0, 1.0, ALU.mult, ALU.add)
            dve.wait_ge(consts, 9)
            link(dve.tensor_reduce(spk[:, 0, 9:10], half[:], AX, ALU.add))
            dve.tensor_copy(spk[:, 1, 9:10], spk[:, 0, 9:10])
            dve.tensor_scalar(spk[:, :, 10:11], spk[:, 0, 9:10].unsqueeze(1).broadcast_to([P, KC, 1]), -1.0, 1.0, ALU.mult, ALU.add)
            dve.tensor_scalar(spk[:, :, 11:12], spk[:, 0, 9:10].unsqueeze(1).broadcast_to([P, KC, 1]), sc[:, 0:1], None, ALU.mult)
            dve.tensor_scalar(spk[:, :, 12:13], spk[:, :, 3:4], sc[:, 1:2], None, ALU.mult)
            link(dve.tensor_scalar(spk[:, :, 13:14], spk[:, :, 2:3], -0.5, None, ALU.mult))
            dve.wait_ge(spl_act, 2)
            link(dve.tensor_scalar(spk[:, :, 14:15], spk[:, :, 5:6], 1e-8, None, ALU.add))
            link(dve.reciprocal(spk[:, :, 15:16], spk[:, :, 14:15]))
            dve.tensor_tensor(spt[:, :, 0, :], spl[:, :, 0, :], spk[:, :, 2:3].broadcast_to([P, KC, HD]), ALU.mult)
            dve.tensor_tensor(spt[:, :, 2, :], spk[:, :, 13:14].broadcast_to([P, KC, HD]),
                              half[:, 0:1].unsqueeze(1).broadcast_to([P, KC, HD]), ALU.bypass)
            link(dve.tensor_tensor(spt[:, :, 1, :], spl[:, :, 1, :], spk[:, :, 15:16].broadcast_to([P, KC, HD]), ALU.mult))
            dve.tensor_tensor(spk[:, :, 6:7], spk[:, :, 8:9], spk[:, :, 13:14], ALU.mult)
            link(dve.tensor_tensor(spsq[:, :, 0, :], spl[:, :, 0, :], spt[:, :, 1, :], ALU.mult))
            link(dve.tensor_reduce(spk[:, :, 4:5], spsq[:, :, 0, :], AX, ALU.add))
            dve.tensor_scalar(spk[:, :, 7:8], spk[:, :, 4:5], -1.0, None, ALU.mult).then_inc(spl_dve, 1)
            for c in range(KC):
                ins = dve.tensor_copy(xs[:, c], spt[:, c].unsqueeze(2).broadcast_to([P, 3, HPC, HD]))
            ins.then_inc(spread, 1)

            n_feat = 0
            for n, use in enumerate(A_USES):
                kind, bank = use[0], n % 8
                if "d" in A_READ[kind]:
                    dve.wait_ge(a_pe, n + 1)
                    if "a" in A_READ[kind]:
                        dve.wait_ge(a_act, A_ACT[n + 1])
                if kind == "xt":
                    tok = slice(2 * P * use[1], 2 * P * (use[1] + 1))
                    dve.tensor_tensor(xt_lo[:, :, tok], ps[:, bank, :].rearrange("p (k t) -> p k t", k=KC),
                                      xt_hi[:, :, tok].bitcast(F32), ALU.subtract).then_inc(a_dve, 1)
                elif kind == "wt":
                    w = use[1]
                    hi, lo = (w_hi[:, w], w_lo[:, w]) if w < 3 else (wo_hi[:], wo_lo[:])
                    dve.tensor_tensor(lo, ps[:, bank, :].rearrange("p (k t) -> p k t", k=KC), hi.bitcast(F32),
                                      ALU.subtract).then_inc(a_dve, 1)
                elif kind == "bt":
                    dve.tensor_copy(bt[:, use[1]], ps[:, bank, 0:3 * P].rearrange("p (j f) -> p j f", j=3)).then_inc(a_dve, 1)
                elif kind == "proj":
                    _, w, hf, c = use
                    cols = slice(hf * BANK, hf * BANK + BANK)
                    if w == 1:
                        dve.wait_ge(a_pe, a_index[("dirp", 0, hf, c)] + 1)
                    dve.tensor_copy(lin[:, c, cols], ps[:, bank, :])
                    dve.scalar_tensor_tensor(out=base_lo[w][:, c, cols], in0=ps[:, bank, :],
                                             scalar=SCALE if w == 0 else 1.0, in1=base_hi[w][:, c, cols].bitcast(F32),
                                             op0=ALU.mult, op1=ALU.subtract).then_inc(a_dve, 1)
                elif kind == "dirp":
                    _, w, hf, c = use
                    cols = slice(hf * BANK, hf * BANK + BANK)
                    dve.wait_ge(a_act, A_ACT[n + 1])
                    link(dve.tensor_scalar(dirp[:, c, cols], dirp[:, c, cols], spk[:, c, 11 if w == 0 else 9:][:, 0:1],
                                           spk[:, c, 10:11], ALU.mult, ALU.add))
                    if w == 0:
                        dve.scalar_tensor_tensor(out=gauss[:, c, cols], in0=gauss[:, c, cols], scalar=spk[:, c, 12:13],
                                                 in1=dirp[:, c, cols], op0=ALU.mult, op1=ALU.mult).then_inc(feat_f, 1)
                    else:
                        dve.tensor_tensor(gauss[:, c, cols], gauss[:, c, cols], dirp[:, c, cols], ALU.mult).then_inc(feat_f, 1)

            def low_half(kind, b, bank):
                hi, lo = (at_hi, at_lo) if kind == "at" else (yt_hi, yt_lo)
                t = 2 * P * (b % 2 if kind == "at" else b)
                return dve.tensor_tensor(lo[:, :, t:t + 2 * P], ps[:, bank, :].rearrange("p (k t) -> p k t", k=KC),
                                         hi[:, :, t:t + 2 * P].bitcast(F32), ALU.subtract)

            def residual(t, bank):
                return dve.tensor_tensor(y[:, t:t + 2, :], ps[:, bank, :].rearrange("p (t d) -> p t d", t=2),
                                         x_sb[:, t:t + 2, :], ALU.add)

            def variance(tiles, src):
                for t in tiles:
                    ins = dve.bn_stats(stats[:, t, :], src[:, t, :])
                link(ins)
                for t in tiles:
                    ins = dve.bn_aggr(mv[:, t, :], stats[:, t, :])
                link(ins)

            def add_eps(tiles):
                dve.tensor_scalar(rstd[:, tiles, 0:1], mv[:, tiles, 1:2], EPS, None, ALU.add).then_inc(var_ready, 1)

            def normalize(tiles, src, dst, count, done):
                dve.wait_ge(std_ready, count)
                link(dve.reciprocal(rstd[:, tiles, 2:3], rstd[:, tiles, 1:2]))
                for t in range(tiles.start, tiles.stop):
                    dve.tensor_scalar(dst[:, t, :], src[:, t, :], mv[:, t, 0:1], rstd[:, t, 2:3],
                                      ALU.subtract, ALU.mult).then_inc(done, 1)

            r = 0
            for it in vector_items:
                slot = r % NR
                if it[0] == "rows":
                    dve.wait_ge(ring_free, r)
                    for c in range(1, PIECES):
                        t = min(i for i in range(T) if len(row_pieces(i)) > c)
                        link(dve.tensor_tensor(mpart[:, 0, t:T], mpart[:, 0, t:T], mpart[:, c, t:T], ALU.max))
                    plain = mpart[:, 0, :, :, 0].rearrange("p t h -> p h t")
                    guided = mpart[:, 0, :, :, 1].rearrange("p t h -> p h t")
                    dve.tensor_scalar(mdiff[:, 0], plain, -1.0, None, ALU.mult)
                    link(dve.tensor_tensor(mdiff[:, 1], plain, guided, ALU.subtract))
                    if it[1] >= 1:
                        dve.wait_ge(ring_full, ring_at[("turn_max", it[1] - 1)] + 1)
                    link(dve.tensor_copy(mrow[:, :, 0].bitcast(F32R), mdiff[:]))
                    dve.tensor_tensor(mrow[:, :, 1].bitcast(F32R), mdiff[:], mrow[:, :, 0], ALU.subtract).then_inc(rows_ready, 1)
                    continue
                dve.wait_ge(ring_full, r + 1)
                if it[0] == "max":
                    _, p, hh, i, c, v, nv = it
                    n = row_pieces(i)[c][2]
                    dve.tensor_reduce(mpart[:, c, i, hh, v:v + nv],
                                      ps[:, slot, :].rearrange("p (v n) -> p v n", v=nv)[:, :, 0:n],
                                      AX, ALU.max).then_inc(ring_free, 1)
                elif it[0] == "turn_max":
                    if it[1] >= 2:
                        dve.wait_ge(m_loaded, 32 * (it[1] - 1))
                    dve.tensor_copy(m_t[:, it[1] % 2, :], ps[0:64, slot, 0:P]).then_inc(ring_free, 1)
                elif it[0] in ("at", "yt"):
                    dve.wait_ge(half_hi, it[1] + (1 if it[0] == "at" else 3))
                    low_half(it[0], it[1], slot).then_inc(ring_free, 1)
                elif it[0] == "wo":
                    residual(2 * it[1], slot).then_inc(ring_free, 1)
                    dve.wait_ge(ring_free, r + 1)
                    variance([2 * it[1], 2 * it[1] + 1], y)
                    if it[1] == 1:
                        add_eps(slice(0, TPG))
                        normalize(slice(0, TPG), y, y, 1, y_ready)
                else:
                    _, p, g = it
                    sums_v = ps[:, slot, :].rearrange("p (a e) -> p a e", e=32)
                    link(dve.reciprocal(rec[:].unsqueeze(2), sums_v[:, :, HD:HD + 1]))
                    link(dve.tensor_tensor(rw[:], rec[:], blend[:].rearrange("p a v -> p (a v)"), ALU.mult))
                    dve.tensor_tensor(otmp[:].rearrange("p t h v d -> p (t h v) d"), sums_v[:, :, 0:HD],
                                      rw[:].unsqueeze(2).broadcast_to([P, 16, HD]), ALU.mult).then_inc(ring_free, 1)
                    dve.wait_ge(ring_free, r + 1)
                    dst = attn[:, TPG * g:TPG * (g + 1), :].rearrange("p t (h e) -> p t h e", h=KC)
                    dve.tensor_tensor(dst[:, :, :, HD * p:HD * (p + 1)], otmp[:, :, :, 0, :], otmp[:, :, :, 1, :],
                                      ALU.add).then_inc(attn_done, 1)
                r += 1

            n = -1
            for use in F_ORDER:
                kind = use[0]
                if kind == "normed":
                    normalize(slice(TPG, T), y, y, 2, y_ready)
                if kind in ("turned", "normed"):
                    continue
                n += 1
                bank = (n + NR) % 8
                if "d" not in F_READ[kind]:
                    continue
                dve.wait_ge(f_pe, n + 1)
                if "a" in F_READ[kind]:
                    dve.wait_ge(f_act, F_ACT[n + 1])
                if kind in ("at", "yt"):
                    low_half(kind, use[1], bank).then_inc(f_dve, 1)
                elif kind == "wo":
                    t = 2 * use[1]
                    residual(t, bank).then_inc(f_dve, 1)
                    dve.wait_ge(f_dve, F_DVE[n + 1])
                    variance([t, t + 1], y)
                    if use[1] == 3:
                        add_eps(slice(TPG, T))
                elif kind == "up":
                    _, nn, s, c = use
                    u = nn * SETS + s
                    dve.wait_ge(f_act, F_ACT[n])
                    if u >= 2 and c == 0:
                        dve.wait_ge(sparse_lo, 4 * (u - 1))
                    dve.tensor_tensor(hid[:, u % 2, c, :], ps[:, bank, :], sg[:, (4 * u + c) % 2, :],
                                      ALU.mult).then_inc(f_dve, 1)
                    if c == 3:
                        sparsify(dve, link, u)
                else:
                    t = use[1]
                    dve.tensor_tensor(x_sb[:, t, :], ps[:, bank, 0:D], y[:, t, :], ALU.add).then_inc(f_dve, 1)
                    for m, tiles in enumerate(LAST_TILES):
                        if t == tiles.stop - 1:
                            dve.wait_ge(f_dve, F_DVE[n + 1])
                            variance(range(tiles.start, tiles.stop), x_sb)
                            add_eps(tiles)
                            if m >= 1:
                                normalize(LAST_TILES[m - 1], x_sb, x_sb, 2 + m, out_ready)
            normalize(LAST_TILES[-1], x_sb, x_sb, 2 + len(LAST_TILES), out_ready)


_INS = ["L0_attn_hidden_states", "L0_attn_Wq", "L0_attn_Wk", "L0_attn_Wv", "L0_attn_Wo",
        "L0_attn_splat_positions", "L0_attn_splat_directions", "L0_attn_splat_log_scales",
        "L0_attn_splat_log_amplitudes", "L0_attn_directional_strength", "L0_attn_position_sensitivity",
        "L0_attn_gsa_strength", "L0_ffn_w_gate", "L0_ffn_w_up", "L0_ffn_w_down"]


def kernel(**inputs):
    import numpy as _np
    import concourse.bacc as _bacc
    from concourse import mybir as _mybir
    from concourse.bass_utils import run_bass_kernel_spmd as _run

    nc = _bacc.Bacc("TRN2", target_bir_lowering=False, num_devices=1)
    arrays, args = {}, []
    for name in _INS:
        a = _np.ascontiguousarray(inputs[name])
        if a.ndim == 0:
            a = a.reshape(1)
        arrays[f"in_{name}_dram"] = a
        args.append(nc.dram_tensor(f"in_{name}_dram", a.shape, _mybir.dt.from_np(a.dtype), kind="ExternalInput").ap())
    out = nc.dram_tensor("out_0_dram", (1, 1024, 256), _mybir.dt.float32, kind="ExternalOutput").ap()
    build_kernel(nc, *args, out)
    r = _run(nc, [arrays], core_ids=[0])
    return r.results[0]["out_0_dram"]
```

```python
from contextlib import ExitStack

import concourse.bass as bass
from concourse import mybir

F32 = mybir.dt.float32
F32R = mybir.dt.float32r
BF16 = mybir.dt.bfloat16
ALU = mybir.AluOpType
ACT = mybir.ActivationFunctionType
AX = mybir.AxisListType.X

P = 128
BANK = 512
EPS = 1e-5
MASKED = -1e30


def build_kernel(nc, X, WQ, WK, WV, WO, POS, DIR, LSC, LAM, DST, PSE, GSA, WG, WU, WD, OUT):
    _, S, D = X.shape
    H, NS, HD = POS.shape
    I = WG.shape[1]
    T = S // P
    KC = D // P
    PAIRS = H // KC
    HPC = H // KC
    G = S // BANK
    TPG = BANK // P
    SPL = 2 * NS
    assert KC == 2 and SPL == HD and HPC * HD == P and G == 2
    ROWS = 3 * (HD + SPL)
    MROW = ROWS
    SROWS = ROWS + 4
    NB = 3
    NP = 3
    SETS = I // (4 * P)
    HC = I // P
    SCALE = float(HD) ** -0.5

    steps = [(p, g, kt) for p in range(PAIRS) for g in range(G) for kt in range(TPG * (g + 1))]
    SPP = len(steps) // PAIRS

    def q_offset(g, kt):
        return max(0, kt - TPG * g) * P

    HALF = BANK // 2

    def score_parts(g, kt):
        d = q_offset(g, kt)
        if kt < TPG * g:
            cut = [(0, BANK, 0, BANK, None)]
        elif d == 0:
            cut = [(0, HALF, 0, HALF, d), (HALF, HALF, HALF, BANK, None)]
        elif d < HALF:
            cut = [(d, HALF, d, d + HALF, d), (HALF, HALF, d + HALF, BANK, None)]
        else:
            cut = [(HALF, HALF, d, BANK, d)]
        return [(hh, v, *part) for hh in range(KC) for part in cut
                for v in ([(0, 1)] if part[1] <= HALF else [(0,), (1,)])]

    parts = [score_parts(g, kt) for _, g, kt in steps]
    parts_by = [sum(len(x) for x in parts[:s]) for s in range(len(steps) + 1)]

    def row_pieces(i):
        if i == 0:
            return [(0, HALF, P)]
        rest = (i - 1) * P
        wide = rest if rest <= BANK else (BANK if rest % HALF == 0 else rest - HALF)
        return ([((i - 1) * P, HALF, HALF)] + ([(0, max(wide, HALF), wide)] if rest else [])
                + ([(wide, HALF, HALF)] if rest > wide else []))

    PIECES = max(len(row_pieces(i)) for i in range(T))

    def row_items(p):
        return [("max", p, hh, i, c, v, nv) for hh in range(KC) for i in range(T)
                for c, piece in enumerate(row_pieces(i))
                for v, nv in (((0, 2),) if piece[1] <= HALF else ((0, 1), (1, 1)))]

    per_pair = len(row_items(0))
    cost_t = [BANK - min(q_offset(g, kt), BANK // 2) for _, g, kt in steps]
    stream = [it for p in range(PAIRS) for it in row_items(p)]
    cost_m = [nv * row_pieces(i)[c][1] for _, _, _, i, c, _, nv in stream]
    NR = 4
    NSC = 7 - NR
    LEAD = 10
    TURN_LAG = 4
    before = (stream[:per_pair] + [("rows", 0)] + stream[per_pair:per_pair + TURN_LAG] + [("turn_max", 0)]
              + stream[per_pair + TURN_LAG:per_pair + LEAD])
    at_step = [[] for _ in steps]
    sent = per_pair + LEAD
    total_t, total_m = float(sum(cost_t)), float(sum(cost_m))
    m_start, run_t = float(sum(cost_m[:sent])), 0.0
    run_m = m_start
    turn_in = -1
    for s in range(len(steps)):
        run_t += cost_t[s]
        here = at_step[s]
        while sent < len(stream) and run_m - m_start < run_t * total_m / total_t:
            here.append(stream[sent])
            run_m += cost_m[sent]
            sent += 1
            if sent % per_pair == 0:
                here.append(("rows", sent // per_pair - 1))
                turn_in = TURN_LAG
            elif turn_in > 0:
                turn_in -= 1
                if turn_in == 0:
                    here.append(("turn_max", sent // per_pair - 1))
        if sent == len(stream) and turn_in > 0:
            turn_in = 0
            at_step[s + 1].append(("turn_max", PAIRS - 1))
        p, g, kt = steps[s]
        if g == 1 and kt == 1:
            here.append(("turn_out", p, 0))
        if p == PAIRS - 1 and g == 1:
            here += {2: [("at", 0), ("at", 1)], 3: [("wo", 0), ("wo", 1)], 6: [("yt", 0), ("yt", 1)]}.get(kt, [])
        if g == 0 and kt == 3 and p > 0:
            here.append(("turn_out", p - 1, 1))
    assert sent == len(stream) and turn_in <= 0
    after = [("turn_out", PAIRS - 1, 1)]
    vector_items = before + [it for here in at_step for it in here] + after
    ring = [it for it in vector_items if it[0] != "rows"]
    ring_at = {it: r for r, it in enumerate(ring)}

    last_steps = (PAIRS - 1) * SPP
    few = len(ring) - len([it for here in at_step[last_steps:] + [after] for it in here if it[0] != "rows"])
    ring_bank = [r % NR if r < few else r % (NR // 2) for r in range(len(ring))]
    score_bank = [NR + n % NSC if n < parts_by[last_steps] else (NR // 2 + n % (NSC + NR // 2))
                  for n in range(parts_by[-1])]

    def latest(banks, end, bank):
        return max([n + 1 for n in range(end) if banks[n] == bank], default=0)

    with ExitStack() as ctx:
        def sem(name):
            return ctx.enter_context(nc.semaphore(name))

        def sb(name, shape, dt, own=ctx, **kw):
            return own.enter_context(nc.sbuf_tensor(name, shape, dt, **kw))

        ps = ctx.enter_context(nc.psum_tensor("ps", [P, 8, BANK], F32))

        x_sb = sb("x_sb", [P, T, D], F32)
        ident = sb("ident", [P, P], F32)
        ident_bf = sb("ident_bf", [P, P], BF16)
        causal = sb("causal", [P, P], BF16)
        wo_hi = sb("wo_hi", [P, KC, D], F32R)
        wo_lo = sb("wo_lo", [P, KC, D], F32R)
        vx = sb("vx", [P, T, H, 32], F32)
        attn = sb("attn", [P, T, D], F32)
        o_sb = sb("o_sb", [P, 2, BANK], F32)
        mpart = sb("mpart", [P, PIECES, T, KC, 2], F32)
        mdiff = sb("mdiff", [P, 2, KC, T], F32)
        mrow = sb("mrow", [P, 2, 2, KC, T], F32)
        m_t = sb("m_t", [64, 2, P], F32)
        rec = sb("rec", [P, 16], F32)
        rw = sb("rw", [P, 16], F32)
        otmp = sb("otmp", [P, TPG, KC, 2, HD], F32)
        sc = sb("sc", [P, 8], F32)
        blend = sb("blend", [P, 8, 2], F32)
        par = sb("par", [P, 2 * HD + 2], F32)
        spread_rows = sb("spread_rows", [P, KC, HPC, 2, NS], F32)
        spar = sb("spar", [P, KC, 2 * HD + 2], F32)
        spl = spar[:, :, 0:2 * HD].rearrange("p c (j d) -> p c j d", j=2)
        spk = sb("spk", [P, KC, 16], F32)
        spt = sb("spt", [P, KC, 3, HD], F32)
        spsq = sb("spsq", [P, KC, 2, HD], F32)
        half = sb("half", [P, HPC], F32)
        stats = sb("stats", [P, T, 6], F32)
        mv = sb("mv", [P, T, 2], F32)
        rstd = sb("rstd", [P, T, 3], F32)
        first = ExitStack()
        k_st = [sb("k_st0", [P, KC, S], F32R, first)]
        q_st = [sb("q_st0", [P, KC, S], F32R, first)]
        s_st = [sb("s_st0", [P, KC, S], F32R, first)]

        right = ExitStack()
        base_hi = [sb(f"base_hi{n}", [P, KC, S], F32R, right, side="right") for n in "qk"]
        base_lo = [sb(f"base_lo{n}", [P, KC, S], F32R, right, side="right") for n in "qk"]
        feat_hi = [sb(f"feat_hi{n}", [P, KC, S], F32R, right, side="right") for n in "qk"]
        feat_lo = [sb(f"feat_lo{n}", [P, KC, S], F32R, right, side="right") for n in "qk"]
        right.close()
        wg_hi = sb("wg_hi", [P, KC, SETS, 4, P], F32R, side="right")
        wg_lo = sb("wg_lo", [P, KC, SETS, 4, P], F32R, side="right")
        wu_hi = sb("wu_hi", [P, KC, SETS, 4, P], F32R, side="right")
        wu_lo = sb("wu_lo", [P, KC, SETS, 4, P], F32R, side="right")
        wd_hi = sb("wd_hi", [P, HC, D], F32R, side="right")
        wd_lo = sb("wd_lo", [P, HC, D], F32R, side="right")
        unsplit = ExitStack()
        raw = [sb(f"raw{n}", [P, 2 * I], F32, unsplit, side="right") for n in range(2)]
        unsplit.close()
        ht_hi, ht_lo = [None] * 3, [None] * 3
        ht_hi[2] = sb("ht_hi2", [P, 4, BANK], F32R, side="right")
        ht_lo[2] = sb("ht_lo2", [P, 4, BANK], F32R, side="right")

        early = ExitStack()
        w_nat = sb("w_nat", [P, 4, KC, D], F32, early)
        w_hi = sb("w_hi", [P, 3, KC, D], F32R, early)
        w_lo = sb("w_lo", [P, 3, KC, D], F32R, early)
        xt_hi = sb("xt_hi", [P, KC, S], F32R, early)
        xt_lo = sb("xt_lo", [P, KC, S], F32R, early)
        lin = sb("lin", [P, KC, S], F32, early)
        sq = sb("sq", [P, KC, S], F32, early)
        gauss = sb("gauss", [P, KC, S], F32, early)
        dirp = sb("dirp", [P, KC, S], F32, early)
        xs = attn[:].rearrange("p t d -> p (t d)")[:, 0:KC * 3 * P].rearrange(
            "p (c j h d) -> p c j h d", c=KC, j=3, h=HPC)
        bt = sb("bt", [P, KC, 3, P], F32, early)
        early.close()
        mid = ExitStack()
        for n in range(1, NB):
            k_st.append(sb(f"k_st{n}", [P, KC, S], F32R, mid))
            q_st.append(sb(f"q_st{n}", [P, KC, S], F32R, mid))
            s_st.append(sb(f"s_st{n}", [P, KC, S], F32R, mid))
        pr = sb("pr", [P, NP, 4, BANK], F32, mid)
        mid.close()
        first.close()
        y = attn
        yt_hi = sb("yt_hi", [P, KC, S], F32R)
        yt_lo = sb("yt_lo", [P, KC, S], F32R)
        at_hi = sb("at_hi", [P, KC, BANK], F32R)
        at_lo = sb("at_lo", [P, KC, BANK], F32R)
        for n in range(2):
            ht_hi[n] = sb(f"ht_hi{n}", [P, 4, BANK], F32R)
            ht_lo[n] = sb(f"ht_lo{n}", [P, 4, BANK], F32R)
        sg = sb("sg", [P, 4, BANK], F32)
        hid = [sb(f"hid{n}", [P, 4, BANK], F32) for n in range(2)]
        hid.append(vx[:, 4:8].rearrange("p t h e -> p t (h e)"))
        mag = vx[:, 0:4].rearrange("p t h e -> p t (h e)")
        beats = sb("beats", [P, 6, BANK], BF16)
        sums = sb("sums", [P, 4, BANK], BF16)
        wins = sb("wins", [P, 4, BANK], BF16)

        x_loaded = [sem(f"x_loaded{n}") for n in range(2)]
        w_loaded, spl_loaded = sem("w_loaded"), sem("spl_loaded")
        consts = sem("consts")
        ident_cast = sem("ident_cast")
        spl_act, spl_dve = sem("spl_act"), sem("spl_dve")
        spread, by_row = sem("spread"), sem("by_row")
        a_pe, a_act, a_dve = sem("a_pe"), sem("a_act"), sem("a_dve")
        lin_read = sem("lin_read")
        feat_f, feat_h, feat_l = sem("feat_f"), sem("feat_h"), sem("feat_l")
        attn_done = sem("attn_done")
        reused = sem("reused")
        st_loaded = [sem(f"st_loaded{b}") for b in range(NB)]
        m_loaded = sem("m_loaded")
        ring_full, ring_free = sem("ring_full"), sem("ring_free")
        rows_ready = sem("rows_ready")
        s_full, exp_done = sem("s_full"), sem("exp_done")
        pv_done, o_evac = sem("pv_done"), sem("o_evac")
        chain = sem("chain")
        raw_loaded = [sem(f"raw_loaded{n}") for n in range(3)]
        prep = sem("prep")
        half_hi = sem("half_hi")
        f_pe, f_act, f_dve = sem("f_pe"), sem("f_act"), sem("f_dve")
        var_ready, std_ready, y_ready = sem("var_ready"), sem("std_ready"), sem("y_ready")
        mag_ready, compared = sem("mag_ready"), sem("compared")
        summed = sem("summed")
        sparse_ready, sparse_hi, sparse_lo = sem("sparse_ready"), sem("sparse_hi"), sem("sparse_lo")
        out_ready, stored = sem("out_ready"), sem("stored")

        TURNED = 6
        def projections(w):
            return [("proj", w, hf, c) for hf in range(2) for c in range(2)]

        def features(w):
            return [(k, w, hf, c) for hf in range(2) for c in range(2) for k in ("gauss", "dirp")]

        A_USES = ([("xt", b) for b in range(4)] + [("wt", 0), ("wt", 1)] + projections(0)[:2]
                  + [("wt", 2), ("bt", 0), ("bt", 1)] + projections(0)[2:] + features(0)
                  + projections(1) + features(1) + [("v", b) for b in range(4)] + [("wt", 3)])
        A_READ = {"xt": "ad", "wt": "ad", "bt": "d", "proj": "ad", "gauss": "a", "dirp": "a", "v": "a"}
        def units(first, end):
            return [(k, m // (4 * SETS), m // 4 % SETS, m % 4) for m in range(first, end) for k in ("gate", "up")]

        F_ORDER = ([("turned",)] + units(0, 1) + [("at", 2), ("at", 3)] + units(1, 2) + [("wo", 2), ("wo", 3)]
                   + units(2, 3) + [("normed",)] + units(3, 4) + [("yt", 2), ("yt", 3)] + units(4, 8 * SETS)
                   + [("down", t) for t in range(T)])
        F_USES = [u for u in F_ORDER if u[0] not in ("turned", "normed")]
        LAST_TILES = [slice(0, TPG), slice(TPG, T)]
        F_READ = {"at": "ad", "wo": "d", "yt": "ad", "gate": "a", "up": "d", "down": "d"}

        def counted(uses, read, who):
            out = [0]
            for u in uses:
                out.append(out[-1] + (who in read[u[0]]))
            return out

        A_ACT, A_DVE = counted(A_USES, A_READ, "a"), counted(A_USES, A_READ, "d")
        F_ACT, F_DVE = counted(F_USES, F_READ, "a"), counted(F_USES, F_READ, "d")
        a_index = {u: n for n, u in enumerate(A_USES)}
        f_index = {u: n for n, u in enumerate(F_USES)}

        def hidden_count(m):
            return F_DVE[f_index[("up", m // (4 * SETS), m // 4 % SETS, m % 4)] + 1]

        def bank_free(pe, uses, read, acts, dves, act_sem, dve_sem, n):
            if n >= 8:
                if "a" in read[uses[n - 8][0]]:
                    pe.wait_ge(act_sem, acts[n - 7])
                if "d" in read[uses[n - 8][0]]:
                    pe.wait_ge(dve_sem, dves[n - 7])

        block = ctx.enter_context(nc.Block())

        @block.sync
        def _(sp):
            xv = X[0].rearrange("(t p) d -> p t d", p=P)
            sp.dma_start(x_sb[:, 0:4, :], xv[:, 0:4, :]).then_inc(x_loaded[0], 16)
            sp.dma_start(x_sb[:, 4:8, :], xv[:, 4:8, :]).then_inc(x_loaded[1], 16)

            def stack(p, which=range(15)):
                b, r = p % NB, HD * p
                parts = ((q_st[b], base_hi[0], 0), (q_st[b], base_hi[0], 1), (q_st[b], base_lo[0], 2),
                         (s_st[b], base_hi[0], 0), (s_st[b], base_hi[0], 1), (s_st[b], base_lo[0], 2),
                         (q_st[b], feat_hi[0], 3), (q_st[b], feat_hi[0], 4), (q_st[b], feat_lo[0], 5),
                         (k_st[b], base_hi[1], 0), (k_st[b], base_lo[1], 1), (k_st[b], base_hi[1], 2),
                         (k_st[b], feat_hi[1], 3), (k_st[b], feat_lo[1], 4), (k_st[b], feat_hi[1], 5))
                for dst, src, n in (parts[i] for i in which):
                    sp.dma_start(dst[HD * n:HD * n + HD, :, :].bitcast(F32),
                                 src[r:r + HD, :, :].bitcast(F32)).then_inc(st_loaded[b], 16)

            def maxima(p):
                sp.wait_ge(ring_free, ring_at[("turn_max", p)] + 1)
                b = p % NB
                sp.dma_start(q_st[b][MROW:MROW + 4, :, :].bitcast(F32), m_t[0:64, p % 2, :]).then_inc(m_loaded, 16)
                sp.dma_start(s_st[b][MROW:MROW + 2, :, :].bitcast(F32), m_t[0:32, p % 2, :]).then_inc(m_loaded, 16)

            sp.wait_ge(consts, 9)
            for w, base, feature in ((0, range(0, 6), range(6, 9)), (1, range(9, 12), range(12, 15))):
                sp.wait_ge(a_act, A_ACT[a_index[("proj", w, 1, 1)] + 1])
                sp.wait_ge(a_dve, A_DVE[a_index[("proj", w, 1, 1)] + 1])
                stack(0, base)
                sp.wait_ge(feat_h, 4 * (w + 1))
                sp.wait_ge(feat_l, 4 * (w + 1))
                stack(0, feature)
            sp.wait_ge(reused, 2 * (NB - 1))
            stack(1)
            stack(2)
            maxima(0)
            for p in range(PAIRS):
                if p + 1 < PAIRS:
                    maxima(p + 1)
                if p + 3 < PAIRS:
                    sp.wait_ge(s_full, parts_by[SPP * (p + 1)])
                    stack(p + 3)
                if p + 3 == PAIRS - 1:
                    for b in range(NB):
                        sp.wait_ge(st_loaded[b], 16 * 15 * len(range(b, PAIRS, NB)))
                    sp.dma_start(raw[0][:], WG.rearrange("(k p) i -> p k i", p=P)).then_inc(raw_loaded[0], 16)
                    sp.dma_start(raw[1][:], WU.rearrange("(k p) i -> p k i", p=P)).then_inc(raw_loaded[1], 16)
            sp.wait_ge(prep, 8)
            sp.dma_start(raw[0][:], WD.rearrange("(s j c) n -> j s c n", s=SETS, c=4)).then_inc(raw_loaded[2], 16)
            ov = OUT[0].rearrange("(t p) d -> p t d", p=P)
            for t in range(T):
                sp.wait_ge(out_ready, t + 1)
                sp.dma_start(ov[:, t, :], x_sb[:, t, :]).then_inc(stored, 16)
            sp.wait_ge(stored, 16 * T)

        @block.gpsimd
        def _(pool):
            pool.memset(ident[:], 0.0).then_inc(consts, 1)
            pool.wait_ge(consts, 1)
            pool.affine_select(out=ident[:], in_=ident[:], compare_op=ALU.not_equal, fill=1.0, base=0,
                               pattern=[[-1, P]], channel_multiplier=1).then_inc(consts, 1)
            pool.memset(spread_rows[:], 0.0).then_inc(spread, 1)
            pool.wait_ge(spread, 1)
            for c in range(KC):
                pool.affine_select(out=spread_rows[:, c], in_=spread_rows[:, c], compare_op=ALU.not_equal, fill=1.0,
                                   base=-HPC * NS * c, pattern=[[-NS, HPC], [0, 2], [-1, NS]],
                                   channel_multiplier=1).then_inc(spread, 1)
            pool.memset(half[:], 1.0).then_inc(consts, 1)
            pool.wait_ge(consts, 3)
            pool.affine_select(out=half[:], in_=half[:], compare_op=ALU.is_ge, fill=0.0, base=-NS,
                               pattern=[[-HD, HPC]], channel_multiplier=1).then_inc(consts, 1)
            pool.wait_ge(consts, 4)
            pool.affine_select(out=half[:], in_=half[:], compare_op=ALU.is_ge, fill=0.0, base=HD - 1,
                               pattern=[[HD, HPC]], channel_multiplier=-1).then_inc(consts, 1)
            pool.wait_ge(spread, 4)
            blocks = xs.rearrange("p c j h d -> p (c j) h d")
            pool.affine_select(out=blocks, in_=blocks, compare_op=ALU.is_ge, fill=0.0, base=0,
                               pattern=[[0, 6], [-HD, HPC], [0, HD]], channel_multiplier=1).then_inc(spread, 1)
            pool.wait_ge(spread, 5)
            pool.affine_select(out=blocks, in_=blocks, compare_op=ALU.is_ge, fill=0.0, base=HD - 1,
                               pattern=[[0, 6], [HD, HPC], [0, HD]], channel_multiplier=-1).then_inc(spread, 1)
            pool.memset(causal[:], 0.0).then_inc(consts, 1)
            pool.wait_ge(consts, 6)
            pool.affine_select(out=causal[:], in_=causal[:], compare_op=ALU.is_ge, fill=MASKED, base=0,
                               pattern=[[-1, P]], channel_multiplier=1).then_inc(consts, 1)
            pool.memset(s_st[0][:].bitcast(F32), 0.0).then_inc(consts, 1)
            pool.wait_ge(consts, 8)
            pool.memset(k_st[0][ROWS:SROWS].bitcast(F32), 1.0).then_inc(consts, 1)
            pool.wait_ge(consts, 9)
            pool.memset(vx[:, :, :, HD:32], 1.0).then_inc(consts, 1)
            for n in range(8):
                w, hf, c = n // 4, n // 2 % 2, n % 2
                cols = slice(hf * BANK, hf * BANK + BANK)
                pool.wait_ge(feat_h, n + 1)
                pool.tensor_tensor(feat_lo[w][:, c, cols], gauss[:, c, cols], feat_hi[w][:, c, cols].bitcast(F32),
                                   ALU.subtract).then_inc(feat_l, 1)
            pool.wait_ge(a_pe, len(A_USES))
            pool.wait_ge(a_act, A_ACT[-1])
            pool.wait_ge(a_dve, A_DVE[-1])
            pool.wait_ge(feat_l, 8)
            for b in range(1, NB):
                pool.memset(s_st[b][:].bitcast(F32), 0.0).then_inc(reused, 1)
                pool.wait_ge(reused, 2 * b - 1)
                pool.memset(k_st[b][ROWS:SROWS].bitcast(F32), 1.0).then_inc(reused, 1)
                pool.wait_ge(reused, 2 * b)

            def slices():
                for n, (src, hi, lo) in enumerate(((raw[0], wg_hi, wg_lo), (raw[1], wu_hi, wu_lo))):
                    rv = src[:].rearrange("p (k s j c) -> p k s c j", k=KC, s=SETS, c=4)
                    for k in range(KC):
                        for s in range(SETS):
                            yield n, rv[:, k, s], hi[:, k, s], lo[:, k, s]
                rv = raw[0][:].rearrange("p (m n) -> p m n", m=HC)
                for m in range(0, HC, 2):
                    yield 2, rv[:, m:m + 2], wd_hi[:, m:m + 2], wd_lo[:, m:m + 2]

            for m, (n, src, hi, lo) in enumerate(slices()):
                pool.wait_ge(raw_loaded[n], 16)
                pool.tensor_scalar(hi, src, 1.0, 0.0, ALU.mult, ALU.add).then_inc(prep, 1)
                pool.wait_ge(prep, 2 * m + 1)
                pool.tensor_tensor(lo, src, hi.bitcast(F32), ALU.subtract).then_inc(prep, 1)
            for n in range(2):
                for s in range(SETS):
                    u = n * SETS + s
                    for c in range(4):
                        pool.wait_ge(sparse_hi, 4 * u + c + 1)
                        pool.tensor_tensor(ht_lo[u % 3][:, c, :], hid[u % 3][:, c, :],
                                           ht_hi[u % 3][:, c, :].bitcast(F32), ALU.subtract).then_inc(sparse_lo, 1)

        def magnitude(act, m):
            u, c = m // 4, m % 4
            act.wait_ge(f_dve, hidden_count(m))
            if c == 0 and u >= 1:
                act.wait_ge(compared, u)
            act.activation(mag[:, c, :], hid[u % 3][:, c, :], ACT.Abs).then_inc(mag_ready, 1)

        def highs(act, u):
            if u == 3:
                act.wait_ge(f_pe, f_index[("down", TPG - 1)] + 1)
            for c in range(4):
                act.wait_ge(sparse_ready, 4 * u + c + 1)
                act.activation(ht_hi[u % 3][:, c, :], hid[u % 3][:, c, :], ACT.Copy).then_inc(sparse_hi, 1)

        def deviation(act, n, tiles):
            act.wait_ge(var_ready, n)
            act.activation(rstd[:, tiles, 1:2], rstd[:, tiles, 0:1], ACT.Sqrt).then_inc(std_ready, 1)

        def high_half(act, kind, b, bank):
            dst, t = (at_hi, 2 * P * (b % 2)) if kind == "at" else (yt_hi, 2 * P * b)
            return act.activation(dst[:, :, t:t + 2 * P], ps[:, bank, :].rearrange("p (k t) -> p k t", k=KC), ACT.Copy)

        @block.scalar
        def _(act):
            for v, cols in ((POS, slice(0, HD)), (DIR, slice(HD, 2 * HD))):
                act.dma_start(par[:, cols], v.rearrange("h n d -> (h n) d")).then_inc(spl_loaded, 16)
            for v, col in ((LSC, 2 * HD), (LAM, 2 * HD + 1)):
                act.dma_start(par[:, col:col + 1], v.rearrange("h (n o) -> (h n) o", o=1)).then_inc(spl_loaded, 16)
            for j, v in enumerate((DST, PSE, GSA)):
                act.dma_start(sc[:, j:j + 1], bass.AP(tensor=v.tensor, offset=0, ap=[[0, P], [1, 1]])).then_inc(spl_loaded, 16)
            for n, w in enumerate((WQ, WK, WV, WO)):
                act.dma_start(w_nat[:, n], w.rearrange("(c p) d -> p c d", p=P)).then_inc(w_loaded, 16)
            act.wait_ge(spl_loaded, 16 * 7)
            act.wait_ge(spl_dve, 1)
            act.activation(spk[:, :, 2:3], spar[:, :, 2 * HD:2 * HD + 1], ACT.Exp, scale=-2.0)
            act.activation(spk[:, :, 3:4], spar[:, :, 2 * HD + 1:2 * HD + 2], ACT.Exp)
            act.activation(sc[:, 3:4], sc[:, 2:3], ACT.Exp, scale=-1.0).then_inc(spl_act, 1)
            act.wait_ge(spl_dve, 2)
            act.activation(spk[:, :, 5:6], spk[:, :, 4:5], ACT.Sqrt).then_inc(spl_act, 1)

            n_feat = 0
            for n, use in enumerate(A_USES):
                kind, bank = use[0], n % 8
                if "a" not in A_READ[kind]:
                    continue
                act.wait_ge(a_pe, n + 1)
                if kind == "xt":
                    b = use[1]
                    act.activation(xt_hi[:, :, 2 * P * b:2 * P * (b + 1)],
                                   ps[:, bank, :].rearrange("p (k t) -> p k t", k=KC), ACT.Copy).then_inc(a_act, 1)
                elif kind == "wt":
                    w = use[1]
                    dst = w_hi[:, w] if w < 3 else wo_hi[:]
                    act.activation(dst, ps[:, bank, :].rearrange("p (k t) -> p k t", k=KC), ACT.Copy).then_inc(a_act, 1)
                elif kind == "proj":
                    _, w, hf, c = use
                    cols = slice(hf * BANK, hf * BANK + BANK)
                    act.activation(base_hi[w][:, c, cols], ps[:, bank, :], ACT.Copy, scale=SCALE if w == 0 else 1.0)
                    if w == 1:
                        act.wait_ge(a_pe, a_index[("gauss", 0, hf, c)] + 1)
                    act.activation(sq[:, c, cols], ps[:, bank, :], ACT.Square).then_inc(a_act, 1)
                elif kind in ("gauss", "dirp"):
                    _, w, hf, c = use
                    cols = slice(hf * BANK, hf * BANK + BANK)
                    if kind == "gauss":
                        act.wait_ge(spl_dve, 3)
                        if w == 1:
                            act.wait_ge(feat_l, n_feat - 4 + 1)
                        act.activation(gauss[:, c, cols], ps[:, bank, :], ACT.Exp,
                                       bias=spk[:, c, 6:7]).then_inc(a_act, 1)
                    else:
                        if w == 1:
                            act.wait_ge(feat_f, n_feat - 4 + 1)
                        act.activation(dirp[:, c, cols], ps[:, bank, :], ACT.Tanh,
                                       bias=spk[:, c, 7:8]).then_inc(a_act, 1)
                        n_feat += 1
                        if n_feat % 4 != 1:
                            m = n_feat - 2
                            act.wait_ge(feat_f, m + 1)
                            mc = slice(m // 2 % 2 * BANK, (m // 2 % 2 + 1) * BANK)
                            act.activation(feat_hi[m // 4][:, m % 2, mc], gauss[:, m % 2, mc], ACT.Copy).then_inc(feat_h, 1)
                        if n_feat in (4, 8):
                            m = n_feat - 1
                            act.wait_ge(feat_f, m + 1)
                            mc = slice(m // 2 % 2 * BANK, (m // 2 % 2 + 1) * BANK)
                            act.activation(feat_hi[m // 4][:, m % 2, mc], gauss[:, m % 2, mc], ACT.Copy).then_inc(feat_h, 1)
                elif kind == "v":
                    t = 2 * use[1]
                    act.wait_ge(consts, 10)
                    act.activation(vx[:, t:t + 2, :, 0:HD],
                                   ps[:, bank, :].rearrange("p (t h d) -> p t h d", t=2, h=H), ACT.Copy).then_inc(a_act, 1)

            def evacuate(n):
                last = SPP * (n // G) + (TPG if n % G == 0 else SPP)
                act.wait_ge(pv_done, last)
                if n >= 2:
                    act.wait_ge(ring_full, ring_at[("turn_out", (n - 2) // G, n % G)] + 1)
                act.activation(o_sb[:, n % 2, :], ps[:, 7, :], ACT.Copy).then_inc(o_evac, 1)

            act.wait_ge(reused, 2 * (NB - 1))
            for s, (p, g, kt) in enumerate(steps):
                for t, (hh, vs, start, width, first_q, end_q, _) in enumerate(parts[s]):
                    n = parts_by[s] + t
                    act.wait_ge(s_full, n + 1)
                    if s >= NP and t == 0:
                        act.wait_ge(pv_done, s - NP + 1)
                    src = ps[:, score_bank[n], :].rearrange("p (v q) -> p v q", q=width)[:, :, first_q - start:end_q - start]
                    act.activation(pr[:, s % NP, 2 * hh + vs[0]:2 * hh + vs[-1] + 1, first_q:end_q], src,
                                   ACT.Exp).then_inc(exp_done, 1)
                if kt == 0 and s > 0:
                    evacuate(G * p + g - 1)
                if p == PAIRS - 1 and g == 1 and kt == 4:
                    deviation(act, 1, slice(0, TPG))
                for it in at_step[s]:
                    if it[0] in ("at", "yt"):
                        act.wait_ge(ring_full, ring_at[it] + 1)
                        high_half(act, it[0], it[1], ring_bank[ring_at[it]]).then_inc(half_hi, 1)
            evacuate(G * PAIRS - 1)

            made = marked = 0
            n = -1
            for use in F_ORDER:
                kind = use[0]
                if kind == "normed":
                    deviation(act, 2, slice(TPG, T))
                if kind in ("turned", "normed"):
                    continue
                n += 1
                bank = (n + NR) % 8
                if "a" not in F_READ[kind]:
                    continue
                if kind == "yt" and marked < made:
                    magnitude(act, marked)
                    marked += 1
                act.wait_ge(f_pe, n + 1)
                if kind in ("at", "yt"):
                    high_half(act, kind, use[1], bank).then_inc(f_act, 1)
                elif kind == "gate":
                    _, nn, s, c = use
                    u = nn * SETS + s
                    m = 4 * u + c
                    if m >= 4:
                        act.wait_ge(f_dve, hidden_count(m - 4))
                    act.activation(sg[:, m % 4, :], ps[:, bank, :], ACT.Silu).then_inc(f_act, 1)
                    if m > marked:
                        magnitude(act, marked)
                        marked += 1
                    made = m + 1
                    if c == 3 and u >= 1:
                        highs(act, u - 1)
            magnitude(act, 8 * SETS - 1)
            highs(act, 2 * SETS - 1)
            for m, tiles in enumerate(LAST_TILES):
                deviation(act, 3 + m, tiles)

        @block.tensor
        def _(pe):
            def three(out, lhs, rhs, first, last, **kw):
                pe.matmul(out, lhs[0], rhs[0], start=first, stop=False, **kw)
                pe.matmul(out, lhs[0], rhs[1], start=False, stop=False, **kw)
                return pe.matmul(out, lhs[1], rhs[0], start=False, stop=last, **kw)

            pe.wait_ge(consts, 2)
            for _ in range(24):
                pe.transpose(ps[:, 6, 0:P], ident[:], ident[:])
            for n, use in enumerate(A_USES):
                kind, bank = use[0], n % 8
                bank_free(pe, A_USES, A_READ, A_ACT, A_DVE, a_act, a_dve, n)
                if n == 7:
                    pe.wait_ge(spl_dve, 1)
                if n == 0:
                    pe.wait_ge(spl_loaded, 16 * 7)
                    pe.wait_ge(spread, 3)
                    for c in range(KC):
                        mm = pe.matmul(ps[:, 7, c * (2 * HD + 2):(c + 1) * (2 * HD + 2)],
                                       spread_rows[:, c].rearrange("p h f n -> p (h f n)"), par[:], start=True, stop=True)
                    mm.then_inc(by_row, 1)
                if kind == "xt":
                    b = use[1]
                    pe.wait_ge(x_loaded[b // 2], 16)
                    for k in range(KC):
                        for t in range(2):
                            o = (2 * k + t) * P
                            mm = pe.transpose(ps[:, bank, o:o + P], x_sb[:, 2 * b + t, P * k:P * (k + 1)], ident[:])
                elif kind == "wt":
                    w = use[1]
                    pe.wait_ge(w_loaded, 64)
                    for k in range(KC):
                        for c in range(KC):
                            o = (2 * k + c) * P
                            mm = pe.transpose(ps[:, bank, o:o + P], w_nat[:, w, c, P * k:P * (k + 1)], ident[:])
                elif kind == "bt":
                    c = use[1]
                    pe.wait_ge(spread, 6)
                    for j in range(3):
                        mm = pe.transpose(ps[:, bank, j * P:(j + 1) * P],
                                          xs[:, c, j].rearrange("p h d -> p (h d)"), ident[:])
                elif kind == "proj":
                    _, w, hf, c = use
                    cols = slice(hf * BANK, hf * BANK + BANK)
                    dims = slice(P * c, P * c + P)
                    pe.wait_ge(a_dve, A_DVE[max(a_index[("wt", w)], a_index[("xt", 2 * hf + 1)]) + 1])
                    for k in range(KC):
                        mm = three(ps[:, bank, :], (w_hi[:, w, k, dims], w_lo[:, w, k, dims]),
                                   (xt_hi[:, k, cols], xt_lo[:, k, cols]), k == 0, k == KC - 1)
                elif kind == "gauss":
                    _, w, hf, c = use
                    cols = slice(hf * BANK, hf * BANK + BANK)
                    pe.wait_ge(a_dve, A_DVE[a_index[("proj", w, hf, c)] + 1])
                    pe.wait_ge(a_dve, A_DVE[a_index[("bt", 1)] + 1])
                    pe.matmul(ps[:, bank, :], bt[:, c, 0], lin[:, c, cols], start=True, stop=False)
                    mm = pe.matmul(ps[:, bank, :], bt[:, c, 2], sq[:, c, cols], start=False, stop=True)
                elif kind == "dirp":
                    _, w, hf, c = use
                    mm = pe.matmul(ps[:, bank, :], bt[:, c, 1], lin[:, c, hf * BANK:hf * BANK + BANK],
                                   start=True, stop=True)
                elif kind == "v":
                    pe.wait_ge(a_dve, A_DVE[a_index[("wt", 2)] + 1])
                    for j in range(2):
                        t = 2 * use[1] + j
                        tok = slice(P * t, P * t + P)
                        for k in range(KC):
                            mm = three(ps[:, bank, j * D:(j + 1) * D], (xt_hi[:, k, tok], xt_lo[:, k, tok]),
                                       (w_hi[:, 2, k, :], w_lo[:, 2, k, :]), k == 0, k == KC - 1)
                mm.then_inc(a_pe, 1)
            pe.wait_ge(a_act, A_ACT[-1])
            pe.wait_ge(a_dve, A_DVE[-1])
            pe.wait_ge(ident_cast, 1)
            pe.wait_ge(consts, 7)

            def turn_tiles(kind, b, bank):
                src = attn if kind == "at" else y
                for k in range(KC):
                    for t in range(2):
                        o = (2 * k + t) * P
                        mm = pe.transpose(ps[:, bank, o:o + P], src[:, 2 * b + t, P * k:P * (k + 1)], ident[:])
                return mm

            def project_out(b, bank):
                for j in range(2):
                    tok = slice(P * (2 * (b % 2) + j), P * (2 * (b % 2) + j + 1))
                    for k in range(KC):
                        mm = three(ps[:, bank, j * D:(j + 1) * D], (at_hi[:, k, tok], at_lo[:, k, tok]),
                                   (wo_hi[:, k, :], wo_lo[:, k, :]), k == 0, k == KC - 1)
                return mm

            def down(t, u, bank, members=range(4)):
                tok = slice(P * (t % TPG), P * (t % TPG + 1))
                for c in members:
                    m = 4 * (u % SETS) + c
                    mm = three(ps[:, bank, 0:D], (ht_hi[u % 3][:, c, tok], ht_lo[u % 3][:, c, tok]),
                               (wd_hi[:, m, :], wd_lo[:, m, :]), m == 0, m == HC - 1)
                return mm

            def item(it):
                if it[0] == "rows":
                    return
                r = ring_at[it]
                slot = ring_bank[r]
                if latest(ring_bank, r, slot):
                    pe.wait_ge(ring_free, latest(ring_bank, r, slot))
                if it[0] == "max":
                    _, p, hh, i, c, v0, nv = it
                    b = p % NB
                    if hh == 0 and i == 0 and v0 == 0:
                        pe.wait_ge(st_loaded[b], 16 * 15 * (p // NB + 1))
                    first, n, _ = row_pieces(i)[c]
                    for v in range(v0, v0 + nv):
                        at = (v - v0) * n
                        mm = pe.matmul(ps[:, slot, at:at + n], (s_st[b], q_st[b])[v][0:ROWS, hh, i * P:(i + 1) * P],
                                       k_st[b][0:ROWS, hh, first:first + n], start=(v == v0), stop=True,
                                       skip_group_check=(v > v0))
                    if c == 0:
                        both = ps[:, slot, :].rearrange("p (v n) -> p v n", v=2)
                        at = i * P - first
                        mm = pe.matmul(both[:, :, at:at + P], ident_bf[:], causal[:].unsqueeze(1).broadcast_to([P, 2, P]),
                                       start=False, stop=True, skip_group_check=True)
                elif it[0] == "turn_max":
                    p = it[1]
                    pe.wait_ge(rows_ready, p + 1)
                    mm = pe.transpose(ps[0:64, slot, 0:P], mrow[:].rearrange("p a b h t -> p (a b h t)"), ident[:])
                elif it[0] in ("at", "yt"):
                    if it[0] == "at":
                        pe.wait_ge(attn_done, G * PAIRS - 1)
                    else:
                        pe.wait_ge(y_ready, 2 * it[1] + 2)
                    mm = turn_tiles(it[0], it[1], slot)
                elif it[0] == "wo":
                    pe.wait_ge(ring_free, ring_at[("at", it[1])] + 1)
                    mm = project_out(it[1], slot)
                else:
                    _, p, g = it
                    n = G * p + g
                    pe.wait_ge(o_evac, n + 1)
                    for t in range(TPG):
                        mm = pe.transpose(ps[:, slot, t * P:(t + 1) * P], o_sb[:, n % 2, t * P:(t + 1) * P], ident[:])
                mm.then_inc(ring_full, 1)

            def values(s):
                p, g, kt = steps[s]
                off = q_offset(g, kt)
                pe.wait_ge(exp_done, parts_by[s + 1])
                if kt == 0 and s > 0:
                    pe.wait_ge(o_evac, G * p + g)
                for t in range(4):
                    mm = pe.matmul(ps[32 * t:32 * t + 32, 7, off:BANK], vx[:, kt, p + HPC * (t // 2), :],
                                   pr[:, s % NP, t, off:BANK], start=(kt == 0), stop=(kt == TPG * (g + 1) - 1),
                                   skip_group_check=True)
                mm.then_inc(pv_done, 1)

            for it in before:
                item(it)
            def scores(s, t):
                p, g, kt = steps[s]
                b, n = p % NB, parts_by[s] + t
                hh, vs, start, width, _, _, diagonal = parts[s][t]
                bank = score_bank[n]
                if s % SPP == 0 and t == 0:
                    pe.wait_ge(m_loaded, 32 * (p + 1))
                if latest(score_bank, n, bank):
                    pe.wait_ge(exp_done, latest(score_bank, n, bank))
                if bank < NR:
                    pe.wait_ge(ring_free, latest(ring_bank, few, bank))
                for j, v in enumerate(vs):
                    q = g * BANK + start
                    mm = pe.matmul(ps[:, bank, j * width:(j + 1) * width], k_st[b][0:SROWS, hh, kt * P:(kt + 1) * P],
                                   (s_st[b], q_st[b])[v][0:SROWS, hh, q:q + width], start=(j == 0), stop=True,
                                   skip_group_check=(j > 0))
                if diagonal is not None:
                    both = ps[:, bank, :].rearrange("p (v q) -> p v q", v=2)
                    at = diagonal - start
                    mm = pe.matmul(both[:, :, at:at + P], causal[:], ident_bf[:].unsqueeze(1).broadcast_to([P, 2, P]),
                                   start=False, stop=True, skip_group_check=True)
                mm.then_inc(s_full, 1)

            for s in range(len(steps)):
                mine = list(at_step[s])
                for t in range(len(parts[s])):
                    scores(s, t)
                    for _ in range(4 // len(parts[s])):
                        if mine:
                            item(mine.pop(0))
                for it in mine:
                    item(it)
                if s >= 1:
                    values(s - 1)
            values(len(steps) - 1)
            pe.wait_ge(exp_done, parts_by[-1])
            pe.wait_ge(ring_free, ring_at[("yt", 1)] + 1)
            pe.wait_ge(prep, 24)
            n = -1
            for use in F_ORDER:
                kind = use[0]
                if kind == "turned":
                    item(after[-1])
                if kind in ("turned", "normed"):
                    continue
                n += 1
                bank = (n + NR) % 8
                if bank == 7 and n < 8:
                    pe.wait_ge(o_evac, G * PAIRS)
                elif bank < NR and n < 8:
                    pe.wait_ge(ring_free, latest(ring_bank, len(ring), bank))
                bank_free(pe, F_USES, F_READ, F_ACT, F_DVE, f_act, f_dve, n)
                if kind in ("at", "yt"):
                    if kind == "at":
                        pe.wait_ge(attn_done, G * PAIRS)
                    else:
                        pe.wait_ge(y_ready, 2 * use[1] + 2)
                    mm = turn_tiles(kind, use[1], bank)
                elif kind == "wo":
                    pe.wait_ge(f_dve, F_DVE[f_index[("at", use[1])] + 1])
                    mm = project_out(use[1], bank)
                elif kind in ("gate", "up"):
                    _, nn, s, c = use
                    cols = slice(nn * BANK, nn * BANK + BANK)
                    if nn == 1:
                        pe.wait_ge(f_dve, F_DVE[f_index[("yt", 3)] + 1])
                    hi, lo = (wg_hi, wg_lo) if kind == "gate" else (wu_hi, wu_lo)
                    for k in range(KC):
                        mm = three(ps[:, bank, :], (hi[:, k, s, c], lo[:, k, s, c]),
                                   (yt_hi[:, k, cols], yt_lo[:, k, cols]), k == 0, k == KC - 1)
                else:
                    t = use[1]
                    if t < TPG:
                        pe.wait_ge(sparse_lo, 4 * SETS)
                        for u in range(SETS):
                            mm = down(t, u, bank)
                    else:
                        if t == TPG:
                            pe.wait_ge(sparse_lo, 4 * 3)
                            for j in range(TPG):
                                if j > 0:
                                    bank_free(pe, F_USES, F_READ, F_ACT, F_DVE, f_act, f_dve, n + j)
                                down(t + j, 2, (n + j + NR) % 8)
                            for c in range(3):
                                pe.wait_ge(sparse_lo, 4 * 3 + c + 1)
                                for j in range(TPG):
                                    down(t + j, 3, (n + j + NR) % 8, [c])
                            pe.wait_ge(sparse_lo, 4 * 4)
                        mm = down(t, 3, bank, [3])
                mm.then_inc(f_pe, 1)

        def compare(dve, u):
            if u >= 1:
                dve.wait_ge(sparse_ready, 4 * u)
            dve.wait_ge(mag_ready, 4 * u + 4)
            dve.tensor_tensor(beats[:, 0:3, :], mag[:, 0:1, :].broadcast_to([P, 3, BANK]), mag[:, 1:4, :], ALU.is_ge)
            dve.tensor_tensor(beats[:, 3:5, :], mag[:, 1:2, :].broadcast_to([P, 2, BANK]), mag[:, 2:4, :], ALU.is_ge)
            dve.tensor_tensor(beats[:, 5, :], mag[:, 2, :], mag[:, 3, :], ALU.is_ge).then_inc(compared, 1)

        def add_beats(dve, u):
            dve.wait_ge(compared, u + 1)
            dve.tensor_tensor(sums[:, 0:2, :], beats[:, 0:4:3, :], beats[:, 1:5:3, :], ALU.add)
            dve.tensor_tensor(sums[:, 2:4, :], beats[:, 1:3, :], beats[:, 3:5, :], ALU.add).then_inc(summed, 1)

        def add_wins(dve, u):
            dve.wait_ge(summed, 2 * u + 1)
            dve.tensor_tensor(wins[:, 0:4:3, :], sums[:, 0:4:3, :], beats[:, 2:6:3, :], ALU.add)
            dve.tensor_tensor(wins[:, 1:3, :], sums[:, 1:3, :], beats[:, 0:6:5, :], ALU.subtract).then_inc(summed, 1)

        def keep(dve, u):
            h = hid[u % 3]
            dve.wait_ge(summed, 2 * u + 2)
            for c, (limit, op) in enumerate(((2.0, ALU.is_ge), (1.0, ALU.is_ge), (0.0, ALU.is_le), (1.0, ALU.is_le))):
                dve.scalar_tensor_tensor(out=h[:, c, :], in0=wins[:, c, :], scalar=limit, in1=h[:, c, :],
                                         op0=op, op1=ALU.mult).then_inc(sparse_ready, 1)

        @block.vector
        def _(dve):
            links = [0]

            def link(ins, between=None):
                links[0] += 1
                ins.then_inc(chain, 1)
                if between is not None:
                    turned_low(between)
                dve.wait_ge(chain, links[0])

            def turned_low(n):
                kind, b = A_USES[n]
                dve.wait_ge(a_pe, n + 1)
                dve.wait_ge(a_act, A_ACT[n + 1])
                src = ps[:, n % 8, :].rearrange("p (k t) -> p k t", k=KC)
                if kind == "xt":
                    hi, lo = xt_hi[:, :, 2 * P * b:2 * P * (b + 1)], xt_lo[:, :, 2 * P * b:2 * P * (b + 1)]
                else:
                    hi, lo = (w_hi[:, b], w_lo[:, b]) if b < 3 else (wo_hi[:], wo_lo[:])
                dve.tensor_tensor(lo, src, hi.bitcast(F32), ALU.subtract).then_inc(a_dve, 1)

            dve.wait_ge(consts, 2)
            dve.tensor_copy(ident_bf[:], ident[:]).then_inc(ident_cast, 1)
            dve.wait_ge(spl_loaded, 16 * 7)
            dve.wait_ge(by_row, 1)
            dve.tensor_copy(spar[:], ps[:, 7, 0:KC * (2 * HD + 2)].rearrange("p (c e) -> p c e", c=KC)).then_inc(spl_dve, 1)
            dve.wait_ge(spl_dve, 1)
            dve.tensor_tensor(spsq[:, :, 1, :], spl[:, :, 1, :], spl[:, :, 1, :], ALU.mult)
            link(dve.tensor_tensor(spsq[:, :, 0, :], spl[:, :, 0, :], spl[:, :, 0, :], ALU.mult))
            dve.wait_ge(spl_act, 1)
            dve.tensor_reduce(spk[:, :, 8:9], spsq[:, :, 0, :], AX, ALU.add)
            dve.tensor_reduce(spk[:, :, 4:5], spsq[:, :, 1, :], AX, ALU.add).then_inc(spl_dve, 1)
            link(dve.tensor_scalar(sc[:, 4:5], sc[:, 3:4], 1.0, None, ALU.add))
            link(dve.reciprocal(sc[:, 5:6], sc[:, 4:5]))
            link(dve.tensor_scalar(sc[:, 6:7], sc[:, 5:6], 0.15, 0.03, ALU.mult, ALU.min), 0)
            dve.tensor_copy(blend[:, :, 1:2], sc[:, 6:7].unsqueeze(1).broadcast_to([P, 8, 1]))
            dve.tensor_scalar(blend[:, :, 0:1], sc[:, 6:7].unsqueeze(1).broadcast_to([P, 8, 1]), -1.0, 1.0, ALU.mult, ALU.add)
            dve.wait_ge(consts, 5)
            link(dve.tensor_reduce(spk[:, 0, 9:10], half[:], AX, ALU.add), 1)
            dve.tensor_copy(spk[:, 1, 9:10], spk[:, 0, 9:10])
            dve.tensor_scalar(spk[:, :, 10:11], spk[:, 0, 9:10].unsqueeze(1).broadcast_to([P, KC, 1]), -1.0, 1.0, ALU.mult, ALU.add)
            dve.tensor_scalar(spk[:, :, 11:12], spk[:, 0, 9:10].unsqueeze(1).broadcast_to([P, KC, 1]), sc[:, 0:1], None, ALU.mult)
            dve.tensor_scalar(spk[:, :, 12:13], spk[:, :, 3:4], sc[:, 1:2], None, ALU.mult)
            link(dve.tensor_scalar(spk[:, :, 13:14], spk[:, :, 2:3], -0.5, None, ALU.mult), 2)
            dve.wait_ge(spl_act, 2)
            link(dve.tensor_scalar(spk[:, :, 14:15], spk[:, :, 5:6], 1e-8, None, ALU.add), 3)
            link(dve.reciprocal(spk[:, :, 15:16], spk[:, :, 14:15]), 4)
            dve.tensor_tensor(spt[:, :, 0, :], spl[:, :, 0, :], spk[:, :, 2:3].broadcast_to([P, KC, HD]), ALU.mult)
            dve.tensor_tensor(spt[:, :, 2, :], spk[:, :, 13:14].broadcast_to([P, KC, HD]),
                              half[:, 0:1].unsqueeze(1).broadcast_to([P, KC, HD]), ALU.bypass)
            link(dve.tensor_tensor(spt[:, :, 1, :], spl[:, :, 1, :], spk[:, :, 15:16].broadcast_to([P, KC, HD]), ALU.mult))
            dve.tensor_tensor(spk[:, :, 6:7], spk[:, :, 8:9], spk[:, :, 13:14], ALU.mult)
            link(dve.tensor_tensor(spsq[:, :, 0, :], spl[:, :, 0, :], spt[:, :, 1, :], ALU.mult))
            link(dve.tensor_reduce(spk[:, :, 4:5], spsq[:, :, 0, :], AX, ALU.add))
            dve.tensor_scalar(spk[:, :, 7:8], spk[:, :, 4:5], -1.0, None, ALU.mult).then_inc(spl_dve, 1)
            for c in range(KC):
                ins = dve.tensor_copy(xs[:, c], spt[:, c].unsqueeze(2).broadcast_to([P, 3, HPC, HD]))
            ins.then_inc(spread, 1)
            for n in range(5, TURNED):
                turned_low(n)

            n_feat = 0
            for n, use in enumerate(A_USES):
                kind, bank = use[0], n % 8
                if n < TURNED:
                    continue
                if "d" in A_READ[kind]:
                    dve.wait_ge(a_pe, n + 1)
                    if "a" in A_READ[kind]:
                        dve.wait_ge(a_act, A_ACT[n + 1])
                if kind == "wt" and n >= TURNED:
                    turned_low(n)
                elif kind == "bt":
                    dve.tensor_copy(bt[:, use[1]], ps[:, bank, 0:3 * P].rearrange("p (j f) -> p j f", j=3)).then_inc(a_dve, 1)
                elif kind == "proj":
                    _, w, hf, c = use
                    cols = slice(hf * BANK, hf * BANK + BANK)
                    if w == 1:
                        dve.wait_ge(a_pe, a_index[("dirp", 0, hf, c)] + 1)
                    dve.tensor_copy(lin[:, c, cols], ps[:, bank, :])
                    dve.scalar_tensor_tensor(out=base_lo[w][:, c, cols], in0=ps[:, bank, :],
                                             scalar=SCALE if w == 0 else 1.0, in1=base_hi[w][:, c, cols].bitcast(F32),
                                             op0=ALU.mult, op1=ALU.subtract).then_inc(a_dve, 1)
                elif kind == "dirp":
                    _, w, hf, c = use
                    cols = slice(hf * BANK, hf * BANK + BANK)
                    dve.wait_ge(a_act, A_ACT[n + 1])
                    link(dve.tensor_scalar(dirp[:, c, cols], dirp[:, c, cols], spk[:, c, 11 if w == 0 else 9:][:, 0:1],
                                           spk[:, c, 10:11], ALU.mult, ALU.add))
                    if w == 0:
                        dve.scalar_tensor_tensor(out=gauss[:, c, cols], in0=gauss[:, c, cols], scalar=spk[:, c, 12:13],
                                                 in1=dirp[:, c, cols], op0=ALU.mult, op1=ALU.mult).then_inc(feat_f, 1)
                    else:
                        dve.tensor_tensor(gauss[:, c, cols], gauss[:, c, cols], dirp[:, c, cols], ALU.mult).then_inc(feat_f, 1)

            def low_half(kind, b, bank):
                hi, lo = (at_hi, at_lo) if kind == "at" else (yt_hi, yt_lo)
                t = 2 * P * (b % 2 if kind == "at" else b)
                return dve.tensor_tensor(lo[:, :, t:t + 2 * P], ps[:, bank, :].rearrange("p (k t) -> p k t", k=KC),
                                         hi[:, :, t:t + 2 * P].bitcast(F32), ALU.subtract)

            def residual(t, bank):
                return dve.tensor_tensor(y[:, t:t + 2, :], ps[:, bank, :].rearrange("p (t d) -> p t d", t=2),
                                         x_sb[:, t:t + 2, :], ALU.add)

            def variance(tiles, src):
                for t in tiles:
                    ins = dve.bn_stats(stats[:, t, :], src[:, t, :])
                link(ins)
                for t in tiles:
                    ins = dve.bn_aggr(mv[:, t, :], stats[:, t, :])
                link(ins)

            def add_eps(tiles):
                dve.tensor_scalar(rstd[:, tiles, 0:1], mv[:, tiles, 1:2], EPS, None, ALU.add).then_inc(var_ready, 1)

            def normalize(tiles, src, dst, count, done):
                dve.wait_ge(std_ready, count)
                link(dve.reciprocal(rstd[:, tiles, 2:3], rstd[:, tiles, 1:2]))
                for t in range(tiles.start, tiles.stop):
                    dve.tensor_scalar(dst[:, t, :], src[:, t, :], mv[:, t, 0:1], rstd[:, t, 2:3],
                                      ALU.subtract, ALU.mult).then_inc(done, 1)

            r = 0
            for it in vector_items:
                slot = ring_bank[min(r, len(ring) - 1)]
                if it[0] == "rows":
                    dve.wait_ge(ring_free, r)
                    for c in range(1, PIECES):
                        t = min(i for i in range(T) if len(row_pieces(i)) > c)
                        link(dve.tensor_tensor(mpart[:, 0, t:T], mpart[:, 0, t:T], mpart[:, c, t:T], ALU.max))
                    plain = mpart[:, 0, :, :, 0].rearrange("p t h -> p h t")
                    guided = mpart[:, 0, :, :, 1].rearrange("p t h -> p h t")
                    dve.tensor_scalar(mdiff[:, 0], plain, -1.0, None, ALU.mult)
                    link(dve.tensor_tensor(mdiff[:, 1], plain, guided, ALU.subtract))
                    if it[1] >= 1:
                        dve.wait_ge(ring_full, ring_at[("turn_max", it[1] - 1)] + 1)
                    link(dve.tensor_copy(mrow[:, :, 0].bitcast(F32R), mdiff[:]))
                    dve.tensor_tensor(mrow[:, :, 1].bitcast(F32R), mdiff[:], mrow[:, :, 0], ALU.subtract).then_inc(rows_ready, 1)
                    continue
                dve.wait_ge(ring_full, r + 1)
                if it[0] == "max":
                    _, p, hh, i, c, v, nv = it
                    n = row_pieces(i)[c][2]
                    dve.tensor_reduce(mpart[:, c, i, hh, v:v + nv],
                                      ps[:, slot, :].rearrange("p (v n) -> p v n", v=nv)[:, :, 0:n],
                                      AX, ALU.max).then_inc(ring_free, 1)
                elif it[0] == "turn_max":
                    if it[1] >= 2:
                        dve.wait_ge(m_loaded, 32 * (it[1] - 1))
                    dve.tensor_copy(m_t[:, it[1] % 2, :], ps[0:64, slot, 0:P]).then_inc(ring_free, 1)
                elif it[0] in ("at", "yt"):
                    dve.wait_ge(half_hi, it[1] + (1 if it[0] == "at" else 3))
                    low_half(it[0], it[1], slot).then_inc(ring_free, 1)
                elif it[0] == "wo":
                    residual(2 * it[1], slot).then_inc(ring_free, 1)
                    dve.wait_ge(ring_free, r + 1)
                    variance([2 * it[1], 2 * it[1] + 1], y)
                    if it[1] == 1:
                        add_eps(slice(0, TPG))
                        normalize(slice(0, TPG), y, y, 1, y_ready)
                else:
                    _, p, g = it
                    sums_v = ps[:, slot, :].rearrange("p (a e) -> p a e", e=32)
                    link(dve.reciprocal(rec[:].unsqueeze(2), sums_v[:, :, HD:HD + 1]))
                    link(dve.tensor_tensor(rw[:], rec[:], blend[:].rearrange("p a v -> p (a v)"), ALU.mult))
                    dve.tensor_tensor(otmp[:].rearrange("p t h v d -> p (t h v) d"), sums_v[:, :, 0:HD],
                                      rw[:].unsqueeze(2).broadcast_to([P, 16, HD]), ALU.mult).then_inc(ring_free, 1)
                    dve.wait_ge(ring_free, r + 1)
                    dst = attn[:, TPG * g:TPG * (g + 1), :].rearrange("p t (h e) -> p t h e", h=KC)
                    dve.tensor_tensor(dst[:, :, :, HD * p:HD * (p + 1)], otmp[:, :, :, 0, :], otmp[:, :, :, 1, :],
                                      ALU.add).then_inc(attn_done, 1)
                r += 1

            n = -1
            for use in F_ORDER:
                kind = use[0]
                if kind == "normed":
                    normalize(slice(TPG, T), y, y, 2, y_ready)
                if kind in ("turned", "normed"):
                    continue
                n += 1
                bank = (n + NR) % 8
                if "d" not in F_READ[kind]:
                    continue
                dve.wait_ge(f_pe, n + 1)
                if "a" in F_READ[kind]:
                    dve.wait_ge(f_act, F_ACT[n + 1])
                if kind in ("at", "yt"):
                    low_half(kind, use[1], bank).then_inc(f_dve, 1)
                elif kind == "wo":
                    t = 2 * use[1]
                    residual(t, bank).then_inc(f_dve, 1)
                    dve.wait_ge(f_dve, F_DVE[n + 1])
                    variance([t, t + 1], y)
                    if use[1] == 3:
                        add_eps(slice(TPG, T))
                elif kind == "up":
                    _, nn, s, c = use
                    u = nn * SETS + s
                    dve.wait_ge(f_act, F_ACT[n])
                    if u >= 3 and c == 0:
                        dve.wait_ge(sparse_lo, 4 * (u - 2))
                    dve.tensor_tensor(hid[u % 3][:, c, :], ps[:, bank, :], sg[:, c, :],
                                      ALU.mult).then_inc(f_dve, 1)
                    if c < 3 and u >= 1:
                        (add_beats, add_wins, keep)[c](dve, u - 1)
                    if c == 3:
                        compare(dve, u)
                    if (u, c) == (2 * SETS - 1, 3):
                        add_beats(dve, u)
                        add_wins(dve, u)
                        keep(dve, u)
                else:
                    t = use[1]
                    dve.tensor_tensor(x_sb[:, t, :], ps[:, bank, 0:D], y[:, t, :], ALU.add).then_inc(f_dve, 1)
                    for m, tiles in enumerate(LAST_TILES):
                        if t == tiles.stop - 1:
                            dve.wait_ge(f_dve, F_DVE[n + 1])
                            variance(range(tiles.start, tiles.stop), x_sb)
                            add_eps(tiles)
                            if m >= 1:
                                normalize(LAST_TILES[m - 1], x_sb, x_sb, 2 + m, out_ready)
            normalize(LAST_TILES[-1], x_sb, x_sb, 2 + len(LAST_TILES), out_ready)


_INS = ["L0_attn_hidden_states", "L0_attn_Wq", "L0_attn_Wk", "L0_attn_Wv", "L0_attn_Wo",
        "L0_attn_splat_positions", "L0_attn_splat_directions", "L0_attn_splat_log_scales",
        "L0_attn_splat_log_amplitudes", "L0_attn_directional_strength", "L0_attn_position_sensitivity",
        "L0_attn_gsa_strength", "L0_ffn_w_gate", "L0_ffn_w_up", "L0_ffn_w_down"]


def kernel(**inputs):
    import numpy as _np
    import concourse.bacc as _bacc
    from concourse import mybir as _mybir
    from concourse.bass_utils import run_bass_kernel_spmd as _run

    nc = _bacc.Bacc("TRN2", target_bir_lowering=False, num_devices=1)
    arrays, args = {}, []
    for name in _INS:
        a = _np.ascontiguousarray(inputs[name])
        if a.ndim == 0:
            a = a.reshape(1)
        arrays[f"in_{name}_dram"] = a
        args.append(nc.dram_tensor(f"in_{name}_dram", a.shape, _mybir.dt.from_np(a.dtype), kind="ExternalInput").ap())
    out = nc.dram_tensor("out_0_dram", (1, 1024, 256), _mybir.dt.float32, kind="ExternalOutput").ap()
    build_kernel(nc, *args, out)
    r = _run(nc, [arrays], core_ids=[0])
    return r.results[0]["out_0_dram"]
```
